# Optimizing a Trainium2 kernel written in Bass

```python
import numpy as np
import jax
import jax.numpy as jnp

def _softmax(x, axis=-1):
    return jax.nn.softmax(x, axis=axis)

def _gelu(x):
    return jax.nn.gelu(x, approximate=True)

def _silu(x):
    return jax.nn.silu(x)

def _sigmoid(x):
    return jax.nn.sigmoid(x)

def _layernorm(x, axis=-1, eps=1e-05):
    m = jnp.mean(x, axis=axis, keepdims=True)
    v = jnp.var(x, axis=axis, keepdims=True)
    return (x - m) / jnp.sqrt(v + eps)

def _scatter_add(tgt, idx, src, axis=0):
    return tgt.at[idx].add(src)

def _segment_sum(src, seg, n):
    return jax.ops.segment_sum(src, seg, n)
kernel_name = 'mk_dlrm_tower_d1_rec_r8_135d03'

def setup_inputs(seed: int=0):
    np.random.seed(seed)
    _w = jnp.asarray

    def _rec_inputs():
        import jax
        import jax.numpy as jnp
        _tk = jax.random.key(seed)
        dense_ctx = jax.random.normal(jax.random.fold_in(_tk, 190), (1024, 16), jnp.float32)
        ids = jnp.stack([jax.random.randint(jax.random.fold_in(_tk, 200 + f), (1024,), 0, v, jnp.int32) for f, v in enumerate([1000, 12500, 1000, 1000, 1250, 12500, 1250, 1000, 1250, 12500, 1000, 12500, 1250, 1250, 1250, 1250, 1000, 1000, 12500, 1000, 1000, 1000, 1250, 1000, 1000, 1000, 1250, 1000, 12500, 1000, 1000, 1250, 1000, 1000, 1000, 1250, 1250, 1250, 1000, 1250, 1000, 1250, 1250, 1250, 1000, 1000, 1250, 1250, 1250, 1250])], axis=1)
        tbl_0 = 0.05 * jax.random.normal(jax.random.fold_in(_tk, 500 + 0), (1000, 300), jnp.float32)
        tbl_1 = 0.05 * jax.random.normal(jax.random.fold_in(_tk, 500 + 1), (12500, 300), jnp.float32)
        tbl_2 = 0.05 * jax.random.normal(jax.random.fold_in(_tk, 500 + 2), (1000, 300), jnp.float32)
        tbl_3 = 0.05 * jax.random.normal(jax.random.fold_in(_tk, 500 + 3), (1000, 300), jnp.float32)
        tbl_4 = 0.05 * jax.random.normal(jax.random.fold_in(_tk, 500 + 4), (1250, 300), jnp.float32)
        tbl_5 = 0.05 * jax.random.normal(jax.random.fold_in(_tk, 500 + 5), (12500, 300), jnp.float32)
        tbl_6 = 0.05 * jax.random.normal(jax.random.fold_in(_tk, 500 + 6), (1250, 300), jnp.float32)
        tbl_7 = 0.05 * jax.random.normal(jax.random.fold_in(_tk, 500 + 7), (1000, 300), jnp.float32)
        tbl_8 = 0.05 * jax.random.normal(jax.random.fold_in(_tk, 500 + 8), (1250, 300), jnp.float32)
        tbl_9 = 0.05 * jax.random.normal(jax.random.fold_in(_tk, 500 + 9), (12500, 300), jnp.float32)
        tbl_10 = 0.05 * jax.random.normal(jax.random.fold_in(_tk, 500 + 10), (1000, 300), jnp.float32)
        tbl_11 = 0.05 * jax.random.normal(jax.random.fold_in(_tk, 500 + 11), (12500, 300), jnp.float32)
        tbl_12 = 0.05 * jax.random.normal(jax.random.fold_in(_tk, 500 + 12), (1250, 300), jnp.float32)
        tbl_13 = 0.05 * jax.random.normal(jax.random.fold_in(_tk, 500 + 13), (1250, 300), jnp.float32)
        tbl_14 = 0.05 * jax.random.normal(jax.random.fold_in(_tk, 500 + 14), (1250, 300), jnp.float32)
        tbl_15 = 0.05 * jax.random.normal(jax.random.fold_in(_tk, 500 + 15), (1250, 300), jnp.float32)
        tbl_16 = 0.05 * jax.random.normal(jax.random.fold_in(_tk, 500 + 16), (1000, 300), jnp.float32)
        tbl_17 = 0.05 * jax.random.normal(jax.random.fold_in(_tk, 500 + 17), (1000, 300), jnp.float32)
        tbl_18 = 0.05 * jax.random.normal(jax.random.fold_in(_tk, 500 + 18), (12500, 300), jnp.float32)
        tbl_19 = 0.05 * jax.random.normal(jax.random.fold_in(_tk, 500 + 19), (1000, 300), jnp.float32)
        tbl_20 = 0.05 * jax.random.normal(jax.random.fold_in(_tk, 500 + 20), (1000, 300), jnp.float32)
        tbl_21 = 0.05 * jax.random.normal(jax.random.fold_in(_tk, 500 + 21), (1000, 300), jnp.float32)
        tbl_22 = 0.05 * jax.random.normal(jax.random.fold_in(_tk, 500 + 22), (1250, 300), jnp.float32)
        tbl_23 = 0.05 * jax.random.normal(jax.random.fold_in(_tk, 500 + 23), (1000, 300), jnp.float32)
        tbl_24 = 0.05 * jax.random.normal(jax.random.fold_in(_tk, 500 + 24), (1000, 300), jnp.float32)
        tbl_25 = 0.05 * jax.random.normal(jax.random.fold_in(_tk, 500 + 25), (1000, 300), jnp.float32)
        tbl_26 = 0.05 * jax.random.normal(jax.random.fold_in(_tk, 500 + 26), (1250, 300), jnp.float32)
        tbl_27 = 0.05 * jax.random.normal(jax.random.fold_in(_tk, 500 + 27), (1000, 300), jnp.float32)
        tbl_28 = 0.05 * jax.random.normal(jax.random.fold_in(_tk, 500 + 28), (12500, 300), jnp.float32)
        tbl_29 = 0.05 * jax.random.normal(jax.random.fold_in(_tk, 500 + 29), (1000, 300), jnp.float32)
        tbl_30 = 0.05 * jax.random.normal(jax.random.fold_in(_tk, 500 + 30), (1000, 300), jnp.float32)
        tbl_31 = 0.05 * jax.random.normal(jax.random.fold_in(_tk, 500 + 31), (1250, 300), jnp.float32)
        tbl_32 = 0.05 * jax.random.normal(jax.random.fold_in(_tk, 500 + 32), (1000, 300), jnp.float32)
        tbl_33 = 0.05 * jax.random.normal(jax.random.fold_in(_tk, 500 + 33), (1000, 300), jnp.float32)
        tbl_34 = 0.05 * jax.random.normal(jax.random.fold_in(_tk, 500 + 34), (1000, 300), jnp.float32)
        tbl_35 = 0.05 * jax.random.normal(jax.random.fold_in(_tk, 500 + 35), (1250, 300), jnp.float32)
        tbl_36 = 0.05 * jax.random.normal(jax.random.fold_in(_tk, 500 + 36), (1250, 300), jnp.float32)
        tbl_37 = 0.05 * jax.random.normal(jax.random.fold_in(_tk, 500 + 37), (1250, 300), jnp.float32)
        tbl_38 = 0.05 * jax.random.normal(jax.random.fold_in(_tk, 500 + 38), (1000, 300), jnp.float32)
        tbl_39 = 0.05 * jax.random.normal(jax.random.fold_in(_tk, 500 + 39), (1250, 300), jnp.float32)
        tbl_40 = 0.05 * jax.random.normal(jax.random.fold_in(_tk, 500 + 40), (1000, 300), jnp.float32)
        tbl_41 = 0.05 * jax.random.normal(jax.random.fold_in(_tk, 500 + 41), (1250, 300), jnp.float32)
        tbl_42 = 0.05 * jax.random.normal(jax.random.fold_in(_tk, 500 + 42), (1250, 300), jnp.float32)
        tbl_43 = 0.05 * jax.random.normal(jax.random.fold_in(_tk, 500 + 43), (1250, 300), jnp.float32)
        tbl_44 = 0.05 * jax.random.normal(jax.random.fold_in(_tk, 500 + 44), (1000, 300), jnp.float32)
        tbl_45 = 0.05 * jax.random.normal(jax.random.fold_in(_tk, 500 + 45), (1000, 300), jnp.float32)
        tbl_46 = 0.05 * jax.random.normal(jax.random.fold_in(_tk, 500 + 46), (1250, 300), jnp.float32)
        tbl_47 = 0.05 * jax.random.normal(jax.random.fold_in(_tk, 500 + 47), (1250, 300), jnp.float32)
        tbl_48 = 0.05 * jax.random.normal(jax.random.fold_in(_tk, 500 + 48), (1250, 300), jnp.float32)
        tbl_49 = 0.05 * jax.random.normal(jax.random.fold_in(_tk, 500 + 49), (1250, 300), jnp.float32)
        _rk = jax.random.fold_in(_tk, 7)
        r_label_embedding = -1.64977e-06 + 0.999867 * jax.random.normal(jax.random.fold_in(_rk, 101), (1024, 200, 300), jnp.float32)
        W_top1 = 0.0680414 * jax.random.normal(jax.random.fold_in(_tk, 801), (216, 512), jnp.float32)
        W_top2 = 0.0441942 * jax.random.normal(jax.random.fold_in(_tk, 802), (512, 256), jnp.float32)
        W_top3 = 0.0625 * jax.random.normal(jax.random.fold_in(_tk, 803), (256, 1), jnp.float32)
        b_top1 = jnp.zeros((512,), jnp.float32)
        b_top2 = jnp.zeros((256,), jnp.float32)
        return (dense_ctx, ids, tbl_0, tbl_1, tbl_2, tbl_3, tbl_4, tbl_5, tbl_6, tbl_7, tbl_8, tbl_9, tbl_10, tbl_11, tbl_12, tbl_13, tbl_14, tbl_15, tbl_16, tbl_17, tbl_18, tbl_19, tbl_20, tbl_21, tbl_22, tbl_23, tbl_24, tbl_25, tbl_26, tbl_27, tbl_28, tbl_29, tbl_30, tbl_31, tbl_32, tbl_33, tbl_34, tbl_35, tbl_36, tbl_37, tbl_38, tbl_39, tbl_40, tbl_41, tbl_42, tbl_43, tbl_44, tbl_45, tbl_46, tbl_47, tbl_48, tbl_49, r_label_embedding, W_top1, b_top1, W_top2, b_top2, W_top3)
    dense_ctx, ids, tbl_0, tbl_1, tbl_2, tbl_3, tbl_4, tbl_5, tbl_6, tbl_7, tbl_8, tbl_9, tbl_10, tbl_11, tbl_12, tbl_13, tbl_14, tbl_15, tbl_16, tbl_17, tbl_18, tbl_19, tbl_20, tbl_21, tbl_22, tbl_23, tbl_24, tbl_25, tbl_26, tbl_27, tbl_28, tbl_29, tbl_30, tbl_31, tbl_32, tbl_33, tbl_34, tbl_35, tbl_36, tbl_37, tbl_38, tbl_39, tbl_40, tbl_41, tbl_42, tbl_43, tbl_44, tbl_45, tbl_46, tbl_47, tbl_48, tbl_49, r_label_embedding, W_top1, b_top1, W_top2, b_top2, W_top3 = _rec_inputs()

    def _L0_rec_setup():
        import jax, jax.numpy as jnp
        import numpy as np
        E, U, C, T, N, B, K = (300, 300, 4, 8, 50, 512, 200)
        P = E * (E - 1) // 2
        PAD = jnp.float32(-2 ** 32 + 1)

        def _attn_pool(x, mask, w_a, b_a, w_b):
            score = jnp.exp((x @ w_a + b_a) @ w_b)
            score = jnp.where(mask == 0, PAD, score)
            p = jax.nn.softmax(score, axis=1)
            return jnp.einsum('bne,bn->be', x, p[..., 0])
        key = jax.random.key(seed)
        ks = jax.random.split(key, 20)
        s = 0.02
        return {'x': jax.random.normal(ks[0], (B, N, E), jnp.float32), 'label_embedding': jax.random.normal(ks[1], (B, K, U), jnp.float32), 'w1': jax.random.normal(ks[2], (E, T), jnp.float32) * s, 'b1': jnp.zeros((T,), jnp.float32), 'w2': jax.random.normal(ks[3], (T, 1), jnp.float32) * s, 'w3': jax.random.normal(ks[4], (E, T), jnp.float32) * s, 'b3': jnp.zeros((T,), jnp.float32), 'w4': jax.random.normal(ks[5], (T, 1), jnp.float32) * s, 'w5': jax.random.normal(ks[6], (2 * E, E), jnp.float32) * s, 'b5': jnp.zeros((E,), jnp.float32), 'w6': jax.random.normal(ks[7], (E, E), jnp.float32) * s, 'b6': jnp.zeros((E,), jnp.float32), 'w7': jax.random.normal(ks[8], (P, E), jnp.float32) * s, 'b7': jnp.zeros((E,), jnp.float32), 'w8': jax.random.normal(ks[9], (2 * E, U), jnp.float32) * s, 'b8': jnp.zeros((U,), jnp.float32), 'v': jax.random.uniform(ks[10], (E, C), jnp.float32)}
    _L0_rec_all = _L0_rec_setup()
    _L0_rec_in = {k: v for k, v in _L0_rec_all.items() if k in ('w1', 'b1', 'w2', 'w3', 'b3', 'w4', 'w5', 'b5', 'w6', 'b6', 'w7', 'b7', 'w8', 'b8', 'v')}
    del _L0_rec_all
    return {'dense_ctx': dense_ctx, 'ids': ids, 'tbl_0': tbl_0, 'tbl_1': tbl_1, 'tbl_2': tbl_2, 'tbl_3': tbl_3, 'tbl_4': tbl_4, 'tbl_5': tbl_5, 'tbl_6': tbl_6, 'tbl_7': tbl_7, 'tbl_8': tbl_8, 'tbl_9': tbl_9, 'tbl_10': tbl_10, 'tbl_11': tbl_11, 'tbl_12': tbl_12, 'tbl_13': tbl_13, 'tbl_14': tbl_14, 'tbl_15': tbl_15, 'tbl_16': tbl_16, 'tbl_17': tbl_17, 'tbl_18': tbl_18, 'tbl_19': tbl_19, 'tbl_20': tbl_20, 'tbl_21': tbl_21, 'tbl_22': tbl_22, 'tbl_23': tbl_23, 'tbl_24': tbl_24, 'tbl_25': tbl_25, 'tbl_26': tbl_26, 'tbl_27': tbl_27, 'tbl_28': tbl_28, 'tbl_29': tbl_29, 'tbl_30': tbl_30, 'tbl_31': tbl_31, 'tbl_32': tbl_32, 'tbl_33': tbl_33, 'tbl_34': tbl_34, 'tbl_35': tbl_35, 'tbl_36': tbl_36, 'tbl_37': tbl_37, 'tbl_38': tbl_38, 'tbl_39': tbl_39, 'tbl_40': tbl_40, 'tbl_41': tbl_41, 'tbl_42': tbl_42, 'tbl_43': tbl_43, 'tbl_44': tbl_44, 'tbl_45': tbl_45, 'tbl_46': tbl_46, 'tbl_47': tbl_47, 'tbl_48': tbl_48, 'tbl_49': tbl_49, 'r_label_embedding': r_label_embedding, 'W_top1': W_top1, 'b_top1': b_top1, 'W_top2': W_top2, 'b_top2': b_top2, 'W_top3': W_top3, 'L0_rec_w1': _L0_rec_in['w1'], 'L0_rec_b1': _L0_rec_in['b1'], 'L0_rec_w2': _L0_rec_in['w2'], 'L0_rec_w3': _L0_rec_in['w3'], 'L0_rec_b3': _L0_rec_in['b3'], 'L0_rec_w4': _L0_rec_in['w4'], 'L0_rec_w5': _L0_rec_in['w5'], 'L0_rec_b5': _L0_rec_in['b5'], 'L0_rec_w6': _L0_rec_in['w6'], 'L0_rec_b6': _L0_rec_in['b6'], 'L0_rec_w7': _L0_rec_in['w7'], 'L0_rec_b7': _L0_rec_in['b7'], 'L0_rec_w8': _L0_rec_in['w8'], 'L0_rec_b8': _L0_rec_in['b8'], 'L0_rec_v': _L0_rec_in['v']}

def reference(dense_ctx, ids, tbl_0, tbl_1, tbl_2, tbl_3, tbl_4, tbl_5, tbl_6, tbl_7, tbl_8, tbl_9, tbl_10, tbl_11, tbl_12, tbl_13, tbl_14, tbl_15, tbl_16, tbl_17, tbl_18, tbl_19, tbl_20, tbl_21, tbl_22, tbl_23, tbl_24, tbl_25, tbl_26, tbl_27, tbl_28, tbl_29, tbl_30, tbl_31, tbl_32, tbl_33, tbl_34, tbl_35, tbl_36, tbl_37, tbl_38, tbl_39, tbl_40, tbl_41, tbl_42, tbl_43, tbl_44, tbl_45, tbl_46, tbl_47, tbl_48, tbl_49, r_label_embedding, W_top1, b_top1, W_top2, b_top2, W_top3, L0_rec_w1, L0_rec_b1, L0_rec_w2, L0_rec_w3, L0_rec_b3, L0_rec_w4, L0_rec_w5, L0_rec_b5, L0_rec_w6, L0_rec_b6, L0_rec_w7, L0_rec_b7, L0_rec_w8, L0_rec_b8, L0_rec_v):
    import jax
    import jax.numpy as jnp

    def _L0_rec_ref(x, label_embedding, w1, b1, w2, w3, b3, w4, w5, b5, w6, b6, w7, b7, w8, b8, v):
        import jax, jax.numpy as jnp
        import numpy as np
        E, U, C, T, N, B, K = (300, 300, 4, 8, 50, 512, 200)
        P = E * (E - 1) // 2
        PAD = jnp.float32(-2 ** 32 + 1)

        def _attn_pool(x, mask, w_a, b_a, w_b):
            score = jnp.exp((x @ w_a + b_a) @ w_b)
            score = jnp.where(mask == 0, PAD, score)
            p = jax.nn.softmax(score, axis=1)
            return jnp.einsum('bne,bn->be', x, p[..., 0])
        mask = jnp.sign(jnp.sum(jnp.abs(x), axis=2))[..., None]
        q1 = _attn_pool(x, mask, w1, b1, w2)
        q2 = _attn_pool(x, mask, w3, b3, w4)
        h = jnp.concatenate([q1, q2], axis=1) @ w5 + b5
        f6 = h @ w6 + b6
        iu, ju = jnp.triu_indices(E, k=1)
        g = (v @ v.T)[iu, ju]
        cross = h[:, iu] * h[:, ju] * g
        f7 = cross @ w7 + b7
        out8 = jnp.concatenate([f6, f7], axis=1) @ w8 + b8
        return jnp.einsum('bu,bku->bk', out8, label_embedding)
    e = jnp.stack([tbl_0[ids[:, 0]], tbl_1[ids[:, 1]], tbl_2[ids[:, 2]], tbl_3[ids[:, 3]], tbl_4[ids[:, 4]], tbl_5[ids[:, 5]], tbl_6[ids[:, 6]], tbl_7[ids[:, 7]], tbl_8[ids[:, 8]], tbl_9[ids[:, 9]], tbl_10[ids[:, 10]], tbl_11[ids[:, 11]], tbl_12[ids[:, 12]], tbl_13[ids[:, 13]], tbl_14[ids[:, 14]], tbl_15[ids[:, 15]], tbl_16[ids[:, 16]], tbl_17[ids[:, 17]], tbl_18[ids[:, 18]], tbl_19[ids[:, 19]], tbl_20[ids[:, 20]], tbl_21[ids[:, 21]], tbl_22[ids[:, 22]], tbl_23[ids[:, 23]], tbl_24[ids[:, 24]], tbl_25[ids[:, 25]], tbl_26[ids[:, 26]], tbl_27[ids[:, 27]], tbl_28[ids[:, 28]], tbl_29[ids[:, 29]], tbl_30[ids[:, 30]], tbl_31[ids[:, 31]], tbl_32[ids[:, 32]], tbl_33[ids[:, 33]], tbl_34[ids[:, 34]], tbl_35[ids[:, 35]], tbl_36[ids[:, 36]], tbl_37[ids[:, 37]], tbl_38[ids[:, 38]], tbl_39[ids[:, 39]], tbl_40[ids[:, 40]], tbl_41[ids[:, 41]], tbl_42[ids[:, 42]], tbl_43[ids[:, 43]], tbl_44[ids[:, 44]], tbl_45[ids[:, 45]], tbl_46[ids[:, 46]], tbl_47[ids[:, 47]], tbl_48[ids[:, 48]], tbl_49[ids[:, 49]]], axis=1)
    z = _L0_rec_ref(e, r_label_embedding, L0_rec_w1, L0_rec_b1, L0_rec_w2, L0_rec_w3, L0_rec_b3, L0_rec_w4, L0_rec_w5, L0_rec_b5, L0_rec_w6, L0_rec_b6, L0_rec_w7, L0_rec_b7, L0_rec_w8, L0_rec_b8, L0_rec_v)
    z = z.reshape(z.shape[0], -1)
    h = jnp.concatenate([z, dense_ctx], axis=1)
    h = jnp.maximum(h @ W_top1 + b_top1, 0.0)
    h = jnp.maximum(h @ W_top2 + b_top2, 0.0)
    y = h @ W_top3
    return y

_drawn_inputs = setup_inputs


def setup_inputs(seed=0):
    import zlib

    import numpy as np

    out = dict(_drawn_inputs(seed))
    spreads = {'b_top1': (0.0, 0.479),
     'b_top2': (0.0, 0.1),
     'L0_rec_b1': (0.0, 0.8),
     'L0_rec_b3': (0.0, 0.8),
     'L0_rec_b5': (0.0, 0.1),
     'L0_rec_b6': (0.0, 0.1),
     'L0_rec_b7': (0.0, 0.1),
     'L0_rec_b8': (0.0, 0.1)}
    factors = {'tbl_0': 8.0,
     'tbl_1': 8.0,
     'tbl_2': 8.0,
     'tbl_3': 8.0,
     'tbl_4': 8.0,
     'tbl_5': 8.0,
     'tbl_6': 8.0,
     'tbl_7': 8.0,
     'tbl_8': 8.0,
     'tbl_9': 8.0,
     'tbl_10': 8.0,
     'tbl_11': 8.0,
     'tbl_12': 8.0,
     'tbl_13': 8.0,
     'tbl_14': 8.0,
     'tbl_15': 8.0,
     'tbl_16': 8.0,
     'tbl_17': 8.0,
     'tbl_18': 8.0,
     'tbl_19': 8.0,
     'tbl_20': 8.0,
     'tbl_21': 8.0,
     'tbl_22': 8.0,
     'tbl_23': 8.0,
     'tbl_24': 8.0,
     'tbl_25': 8.0,
     'tbl_26': 8.0,
     'tbl_27': 8.0,
     'tbl_28': 8.0,
     'tbl_29': 8.0,
     'tbl_30': 8.0,
     'tbl_31': 8.0,
     'tbl_32': 8.0,
     'tbl_33': 8.0,
     'tbl_34': 8.0,
     'tbl_35': 8.0,
     'tbl_36': 8.0,
     'tbl_37': 8.0,
     'tbl_38': 8.0,
     'tbl_39': 8.0,
     'tbl_40': 8.0,
     'tbl_41': 8.0,
     'tbl_42': 8.0,
     'tbl_43': 8.0,
     'tbl_44': 8.0,
     'tbl_45': 8.0,
     'tbl_46': 8.0,
     'tbl_47': 8.0,
     'tbl_48': 8.0,
     'tbl_49': 8.0,
     'L0_rec_w1': 8.0,
     'L0_rec_w2': 8.0,
     'L0_rec_w3': 8.0,
     'L0_rec_w4': 8.0,
     'L0_rec_w5': 4.998}
    for name, (base, spread) in spreads.items():
        noise = np.random.default_rng([zlib.crc32(name.encode()), seed]).standard_normal(out[name].shape)
        drawn = base * np.exp(spread * noise) if base else spread * noise
        out[name] = jnp.asarray(drawn.astype(out[name].dtype))
    for name, factor in factors.items():
        out[name] = (out[name] * factor).astype(out[name].dtype)
    return out
```

```python
from contextlib import ExitStack

import numpy as np

import concourse.bass as bass
from concourse import mybir

F32 = mybir.dt.float32
I32 = mybir.dt.int32
ALU = mybir.AluOpType
ACT = mybir.ActivationFunctionType
AX_X = mybir.AxisListType.X

P = 128
BATCH, FIELDS, EMB, LABELS, RANK, HIDDEN = 1024, 50, 300, 200, 4, 8
CTX, TOP1, TOP2 = 16, 512, 256
TILES = BATCH // P
GT = 2
GROUPS = TILES // GT
GB = GT * P
PAD = float(-2 ** 32 + 1)

DISTANCES = EMB // 2
SHIFTS = 5
BLOCKS = DISTANCES // SHIFTS
CP = 125
CHUNKS = SHIFTS * EMB // CP
CROSS = SHIFTS * EMB
TB = BLOCKS // GT
FG = 10
NFG = FIELDS // FG
SLAB = 8
SLABS = LABELS // SLAB
SLOTS = 3
JUNK = 4
TR = 3
QC, QCN = 120, 2 * EMB // 120
EC, ECN = 100, EMB // 100
ZC, ZCN = 100, LABELS // 100
M1, M2 = TOP1 // P, TOP2 // P

SLABS_AT = [1] * NFG + [1] * NFG + [3] * (TB - 2 * NFG)
FIRST_SLAB = [sum(SLABS_AT[:b]) for b in range(TB)]
assert sum(SLABS_AT) == SLABS
DOTS = 2 * FG
WSUMS = 2 * FIELDS + 4
CHAIN = 7
CONSTS = 17
CREDIT = 2 * CHUNKS


def per_tile(pool, labels):
    return NFG * DOTS * pool + LABELS * labels


def rows_through(block, pool, labels, slab=None):
    n = min(block, NFG) * DOTS * pool + FIRST_SLAB[block] * SLAB * labels
    if slab is not None:
        n += DOTS * pool * (block < NFG) + (slab - FIRST_SLAB[block] + 1) * SLAB
    return n


STAGE_POOLS = [g < GROUPS - 1 for g in range(GROUPS)]
STAGE_LABELS = [g > 0 for g in range(GROUPS)]
ROWS_AT = [JUNK + GT * per_tile(1, 0)]
for _g in range(GROUPS):
    ROWS_AT.append(ROWS_AT[-1] + GT * per_tile(STAGE_POOLS[_g], STAGE_LABELS[_g]))
ROWS_END = ROWS_AT[-1] + GT * LABELS


def dlrm_tower(nc, ids, tables, labels, ctx_t, w_score, b_rep, w5, b5, w6, b67_in, w7, w8, b8,
               v_i, v_j, top1, top1_ctx, bias1, top2, bias2, top3, ident_in, y_out):
    with ExitStack() as ctx:
        def sb(name, shape, dt=F32):
            return ctx.enter_context(nc.sbuf_tensor(name, shape, dt))

        def ps(name, shape):
            return ctx.enter_context(nc.psum_tensor(name, shape, F32))

        def sem(name):
            return ctx.enter_context(nc.semaphore(name))

        ident = sb("ident", [P, P])
        w5_sb = sb("w5_sb", [QC, QCN, EMB])
        w68 = sb("w68", [EC, ECN, EMB])
        w8_sb = sb("w8_sb", [EC, ECN, EMB])
        top1_sb = sb("top1_sb", [ZC, ZCN, TOP1])
        bias1_sb = sb("bias1_sb", [P, M1])
        top2_sb = sb("top2_sb", [P, M1, TOP2])
        bias2_sb = sb("bias2_sb", [P, M2])
        top3_sb = sb("top3_sb", [P, M2])
        pads = sb("pads", [P, FIELDS])
        g_all = sb("g_all", [P, BLOCKS * CHUNKS])
        score_u = sb("score_u", [P, 2, EMB + 1])
        narrow = sb("narrow", [48, BATCH + TOP1])
        b5_sb = narrow[0:1, 0:EMB]
        bias8 = narrow[0:1, EMB:2 * EMB]
        b8_sb = narrow[0:1, 2 * EMB:3 * EMB]
        y_sb = narrow[0:1, BATCH:BATCH + GB]
        ones = narrow[0:1, BATCH + GB:BATCH + GB + P]
        ctx_sb = narrow[32:32 + CTX, 0:BATCH]
        top1c_sb = narrow[32:32 + CTX, BATCH:BATCH + TOP1]
        ids_sb = sb("ids_sb", [P, FIELDS], I32)
        x = sb("x", [P, FIELDS, EMB])
        absum = sb("absum", [P, FIELDS])
        columns = sb("columns", [P, 6, 2])
        top, ntop, exsum, rsum, tick = (columns[:, i, :] for i in range(5))
        abs_junk = sb("abs_junk", [P, 2, EMB], mybir.dt.bfloat16)
        score = sb("score", [P, 2, FIELDS])
        empty = sb("empty", [P, FIELDS], I32)
        ex = sb("ex", [P, 2, FIELDS])
        qa = sb("qa", [P, 2, 2, EMB])
        q = sb("q", [P, GT, 2 * EMB])
        hh = sb("hh", [P, GT, 2 * EMB])
        cross = sb("cross", [P, 2, GT, CROSS])
        w7_sb = sb("w7_sb", [P, 2, CHUNKS * EMB])
        ct = sb("ct", [P, TR, GB])
        ht = sb("ht", [EC, GT, ECN * P])
        out8 = sb("out8", [P, GT, EMB])
        spare = sb("spare", [P, GT * QCN * P])
        qflat = q[:].rearrange("p t n -> p (t n)")
        qt = spare[0:QC, :].rearrange("p (t n) -> p t n", t=GT)
        f7s = qflat[:, 0:GT * EMB].rearrange("p (t e) -> p t e", t=GT)
        f7t = spare[0:EC, 0:GT * ECN * P].rearrange("p (t n) -> p t n", t=GT)
        zt = qflat[0:ZC, 0:ZCN * GB].rearrange("p (c b) -> p c b", c=ZCN)
        h1t = spare[:, 0:M1 * GB].rearrange("p (c b) -> p c b", c=M1)
        h2t = qflat[:, 0:M2 * GB].rearrange("p (c b) -> p c b", c=M2)
        lab = sb("lab", [P, SLOTS, SLAB, EMB])
        start = lab[:].rearrange("p s k e -> p (s k e)")
        at = [0]

        def early(rows, *dims):
            n = int(np.prod(dims))
            view = start[0:rows, at[0]:at[0] + n]
            at[0] += n
            return view.rearrange("p (a b) -> p a b", a=dims[0]) if len(dims) == 2 else view

        score_w = early(HIDDEN, 2, EMB + 1)
        score_v = early(HIDDEN, 2, P)
        w6t = early(EC, ECN, EMB)
        w8a = early(EC, ECN, EMB)
        b67 = early(EC, 2 * ECN)
        junk = sb("junk", [P, JUNK, EMB])
        z = sb("z", [P, 2, GT, LABELS])

        acc = [ps(f"acc{i}", [P, GT, 512]) for i in range(2)]
        turned = [ps(f"turned{i}", [P, 512]) for i in range(TR)]
        misc = ps("misc", [P, 512])

        score_consts = sem("score_consts")
        consts = sem("consts")
        filled = sem("filled")
        g_ready = sem("g_ready")
        ids_loaded = sem("ids_loaded")
        gathered = [sem(f"gathered{j}") for j in range(NFG)]
        abs_done = sem("abs_done")
        pool_ticks = sem("pool_ticks")
        rows_done = sem("rows_done")
        exp1_done = sem("exp1_done")
        chain = sem("chain")
        ntop_ready = sem("ntop_ready")
        exp2_done = sem("exp2_done")
        wsum_done = sem("wsum_done")
        q_ready = sem("q_ready")
        hh_ready = sem("hh_ready")
        cross_ready = sem("cross_ready")
        w7_loaded = [sem(f"w7_loaded{i}") for i in range(2)]
        chunk_turned = sem("chunk_turned")
        chunk_ready = sem("chunk_ready")
        chunk_used = sem("chunk_used")
        pe_step = sem("pe_step")
        act_step = sem("act_step")
        out8_ready = sem("out8_ready")
        lab_loaded = [sem(f"lab_loaded{i}") for i in range(SLOTS)]
        y_ready = sem("y_ready")
        y_stored = sem("y_stored")

        label_rows = labels.rearrange("(t p) k e -> t p (k e)", p=P)
        id_rows = ids.rearrange("(t p) n -> t p n", p=P)

        block = ctx.enter_context(nc.Block())

        @block.sync
        def _(sp):
            sp.dma_start(score_w, w_score).then_inc(score_consts, 16)
            sp.dma_start(score_v, b_rep).then_inc(score_consts, 16)
            sp.dma_start(cross[:, 0, 0, 0:BLOCKS * CHUNKS * RANK], v_i).then_inc(consts, 16)
            sp.dma_start(cross[:, 0, 1, 0:BLOCKS * CHUNKS * RANK], v_j).then_inc(consts, 16)
            for dst, src in ((ident[:], ident_in), (w5_sb[:], w5), (b5_sb, b5), (w6t, w6), (b67, b67_in),
                             (w8a, w8[:, 0:ECN, :]), (w8_sb[:], w8[:, ECN:2 * ECN, :]), (b8_sb, b8),
                             (top1_sb[:], top1), (top1c_sb, top1_ctx), (bias1_sb[:], bias1),
                             (top2_sb[:], top2), (bias2_sb[:], bias2), (top3_sb[:], top3),
                             (ctx_sb, ctx_t)):
                sp.dma_start(dst, src).then_inc(consts, 16)

            def load_w7(gb, b, par, first=False):
                if not first:
                    sp.wait_ge(chunk_used, CHUNKS * (gb - 1))
                sp.dma_start(w7_sb[:, par, :], w7[b]).then_inc(w7_loaded[par], 16)

            def load_slab(tile, s, used):
                sp.wait_ge(rows_done, used)
                sp.dma_start(lab[:, s % SLOTS, :, :].rearrange("p k e -> p (k e)"),
                             label_rows[tile, :, s * SLAB * EMB:(s + 1) * SLAB * EMB]
                             ).then_inc(lab_loaded[s % SLOTS], 16)

            def slot_used(rows0, tile_rows, a, b, s, pool):
                if s < SLOTS:
                    return rows0 + a * tile_rows
                prev = s - SLOTS
                pb = max(i for i in range(TB) if FIRST_SLAB[i] <= prev)
                return rows0 + a * tile_rows + rows_through(pb, pool, 1, prev)

            def stage(g, rows0, pool, with_labels, first=False):
                for a in range(GT):
                    for b in range(TB):
                        gb = a * TB + b
                        load_w7(g * BLOCKS + gb, gb, gb % 2, first=first and gb < 2)
                        for s in range(FIRST_SLAB[b], FIRST_SLAB[b] + SLABS_AT[b]) if with_labels else ():
                            load_slab((g - 1) * GT + a, s,
                                      slot_used(rows0, per_tile(pool, 1), a, b, s, pool))

            load_w7(0, 0, 0, first=True)
            load_w7(1, 1, 1, first=True)
            with sp.Fori(1, BLOCKS // 2) as pair:
                load_w7(2 * pair, 2 * pair, 0)
                load_w7(2 * pair + 1, 2 * pair + 1, 1)
            step = ROWS_AT[2] - ROWS_AT[1]
            with sp.Fori(1, GROUPS - 1) as g:
                stage(g, ROWS_AT[1] - step + g * step, 1, True)
            stage(GROUPS - 1, ROWS_AT[GROUPS - 1], 0, True)
            with sp.Fori(0, GT) as a:
                for s in range(SLABS):
                    used = ROWS_AT[GROUPS] + (s - SLOTS + 1) * SLAB if s >= SLOTS else ROWS_AT[GROUPS]
                    load_slab((GROUPS - 1) * GT + a, s, used + a * LABELS)

        @block.gpsimd
        def _(pool):
            def carry(tile_ticks, i):
                pool.wait_ge(pool_ticks, tile_ticks + i + 1)
                pool.tensor_tensor(tick[:, 1:2], tick[:, 0:1], tick[:, 0:1],
                                   ALU.add).then_inc(pool_ticks, 1)

            def tile(t, first=False):
                pool.dma_start(ids_sb[:], id_rows[t]).then_inc(ids_loaded, 16)
                pool.wait_ge(ids_loaded, 16 * (t + 1))
                carry(0 if first else t * (NFG + 1) - NFG, 0)
                for n in range(FIELDS):
                    j = n // FG
                    if n % FG == 0 and not first:
                        pool.wait_ge(wsum_done, WSUMS * t - 2 * FIELDS + 2 * FG * (j + 1))
                        carry(t * (NFG + 1) - NFG, j + 1)
                    pool.indirect_dma_start(
                        out=x[:, n, :], out_offset=None, in_=tables[n],
                        in_offset=bass.IndirectOffsetOnAxis(ap=ids_sb[:, n:n + 1], axis=0)
                    ).then_inc(gathered[j], 16)
                for j in range(NFG):
                    pool.wait_ge(gathered[j], 16 * FG * (t + 1))

            pool.memset(tick, 0.0).then_inc(pool_ticks, 1)
            tile(0, first=True)
            with pool.Fori(1, TILES) as t:
                tile(t)

        @block.vector
        def _(dve):
            dve.memset(ones, 1.0).then_inc(filled, 1)
            dve.memset(pads[:], PAD).then_inc(filled, 1)
            for r in range(JUNK):
                dve.memset(junk[:, r, :], 0.0).then_inc(rows_done, 1)
            dve.wait_ge(consts, 16 * CONSTS)
            nv = BLOCKS * CHUNKS * RANK
            dve.tensor_tensor(cross[:, 0, 0, 0:nv], cross[:, 0, 0, 0:nv], cross[:, 0, 1, 0:nv],
                              ALU.mult).then_inc(g_ready, 1)
            dve.wait_ge(g_ready, 1)
            dve.tensor_reduce(g_all[:], cross[:, 0, 0, 0:nv].rearrange("p (n r) -> p n r", r=RANK),
                              AX_X, ALU.add).then_inc(g_ready, 1)
            dve.wait_ge(g_ready, 2)
            dve.wait_ge(filled, 2)
            dve.wait_ge(act_step, 1)

            def row(count, i, in0, in1, out):
                dve.wait_ge(rows_done, count - JUNK + 1)
                dve.scalar_tensor_tensor(junk[:, i % JUNK, :], in0, 1.0, in1, ALU.mult, ALU.mult,
                                         accum_out=out).then_inc(rows_done, 1)

            def dots(t, count, j):
                dve.wait_ge(gathered[j], 16 * FG * (t + 1))
                for i in range(DOTS):
                    n, head = j * FG + i // 2, i % 2
                    row(count + i, i, x[:, n, :], score_u[:, head, 0:EMB], score[:, head, n:n + 1])

            def softmax(t):
                c = t * CHAIN

                def then(k):
                    dve.wait_ge(chain, c + k)

                dve.wait_ge(abs_done, FIELDS * (t + 1))
                dve.tensor_scalar(empty[:], absum[:], 0.0, None, ALU.is_equal).then_inc(chain, 1)
                dve.wait_ge(exp1_done, 2 * (t + 1))
                then(1)
                dve.memset(qa[:], 0.0).then_inc(wsum_done, 4)
                for head in range(2):
                    dve.copy_predicated(score[:, head, :], empty[:], pads[:]).then_inc(chain, 1)
                then(3)
                dve.tensor_reduce(top, score[:], AX_X, ALU.max).then_inc(chain, 1)
                then(4)
                dve.tensor_scalar(ntop, top, -1.0, None, ALU.mult).then_inc(ntop_ready, 1)
                dve.wait_ge(exp2_done, 2 * (t + 1))
                dve.reciprocal(rsum, exsum).then_inc(chain, 1)
                then(5)
                for head in range(2):
                    dve.tensor_scalar(ex[:, head, :], ex[:, head, :], rsum[:, head:head + 1], None,
                                      ALU.mult).then_inc(chain, 1)
                then(7)

            def wsums(t, j):
                for i in range(DOTS):
                    n, head = j * FG + i // 2, i % 2
                    dve.wait_ge(wsum_done, WSUMS * t + j * DOTS + i + 1)
                    part = qa[:, n % 2, head, :]
                    dve.scalar_tensor_tensor(part, x[:, n, :], ex[:, head, n:n + 1], part,
                                             ALU.mult, ALU.add).then_inc(wsum_done, 1)

            def pooled(t, a):
                dve.wait_ge(wsum_done, WSUMS * (t + 1))
                dve.tensor_tensor(q[:, a, :].rearrange("p (h e) -> p h e", h=2), qa[:, 0], qa[:, 1],
                                  ALU.add).then_inc(q_ready, 1)
                dve.wait_ge(q_ready, t + 1)

            def make_cross(g, a, b):
                par = a if b % 2 == 0 else 1 - a
                dve.wait_ge(chunk_turned, CREDIT + CHUNKS * (g * BLOCKS + a * TB + b - 1))
                b = a * TB + b
                win = hh[:, :, bass.ds(SHIFTS * b + 1, EMB)]
                shifted = bass.AP(tensor=win.tensor, offset=win.offset,
                                  ap=[list(win.ap[0]), list(win.ap[1]), [1, SHIFTS], [1, EMB]])
                still = hh[:, :, 0:EMB]
                still = bass.AP(tensor=still.tensor, offset=still.offset,
                                ap=[list(still.ap[0]), list(still.ap[1]), [0, SHIFTS], [1, EMB]])
                dst = cross[:, par, :, :].rearrange("p t (s e) -> p t s e", s=SHIFTS)
                dve.tensor_tensor(dst, still, shifted, ALU.mult).then_inc(cross_ready, 1)

            def slab(zp, a, s, loads, count):
                dve.wait_ge(lab_loaded[s % SLOTS], 16 * loads)
                for i in range(SLAB):
                    row(count + i, i, lab[:, s % SLOTS, i, :],
                        out8[:, a, :], z[:, zp, a, s * SLAB + i:s * SLAB + i + 1])

            def slot_loads(tile, s):
                return tile * len(range(s % SLOTS, SLABS, SLOTS)) + s // SLOTS + 1

            def stage(g, pools, with_labels):
                dve.wait_ge(hh_ready, 2 * (g + 1))
                with dve.Fori(0, GT) as a:
                    count = ROWS_AT[g] + a * per_tile(pools, with_labels)
                    t = (g + 1) * GT + a
                    for b in range(TB):
                        if b == 0:
                            make_cross(g, a, 0)
                            make_cross(g, a, 1)
                        here = count + rows_through(b, pools, with_labels)
                        if pools and b < NFG:
                            dots(t, here, b)
                            here = here + DOTS
                        if with_labels:
                            if b == 0:
                                dve.wait_ge(out8_ready, g)
                            for s in range(FIRST_SLAB[b], FIRST_SLAB[b] + SLABS_AT[b]):
                                slab((g - 1) % 2, a, s, slot_loads((g - 1) * GT + a, s), here)
                                here = here + SLAB
                        if pools and b == NFG:
                            softmax(t)
                        if pools and NFG <= b < 2 * NFG:
                            wsums(t, b - NFG)
                        if pools and b == 2 * NFG - 1:
                            pooled(t, a)
                        if b + 2 < TB:
                            make_cross(g, a, b + 2)

            with dve.Fori(0, GT) as a:
                for j in range(NFG):
                    dots(a, JUNK + a * per_tile(1, 0) + j * DOTS, j)
                softmax(a)
                for j in range(NFG):
                    wsums(a, j)
                pooled(a, a)
            dve.engine_nop().then_inc(chunk_turned, CREDIT)
            for g in range(GROUPS):
                stage(g, STAGE_POOLS[g], STAGE_LABELS[g])
            dve.wait_ge(out8_ready, GROUPS)
            with dve.Fori(0, GT) as a:
                for s in range(SLABS):
                    slab((GROUPS - 1) % 2, a, s, slot_loads((GROUPS - 1) * GT + a, s),
                         ROWS_AT[GROUPS] + a * LABELS + s * SLAB)

        class Steps:

            def __init__(self):
                self.pe = self.act = 0

        def bursts_of(stage):
            names = []
            if stage >= 1:
                names += [("f7", stage - 1), ("out8", stage - 1)]
            if stage < GROUPS:
                names += [("ht", stage)]
            if stage >= 2:
                names += [(n, stage - 2) for n in ("zt", "h1", "h2", "y")]
            return names

        @block.tensor
        def _(pe):
            steps = Steps()

            def done(ins):
                ins.then_inc(pe_step, 1)
                steps.pe += 1

            def after_copies(n):
                steps.act += n
                pe.wait_ge(act_step, steps.act)

            def turn(gb, par, c):
                gc = gb * CHUNKS + c
                if not (isinstance(gc, int) and gc < TR):
                    pe.wait_ge(chunk_ready, gc - TR + 1)
                for t in range(GT):
                    last = pe.transpose(turned[c % TR][0:CP, t * P:(t + 1) * P],
                                        cross[:, par, t, c * CP:(c + 1) * CP], ident[:])
                last.then_inc(chunk_turned, 1)

            def through_w7(gc, par, c, g, start=False, stop=False):
                pe.wait_ge(chunk_ready, gc + 1)
                for t in range(GT):
                    last = pe.matmul(acc[g % 2][:, t, 0:EMB], ct[0:CP, c % TR, t * P:(t + 1) * P],
                                     w7_sb[0:CP, par, c * EMB:(c + 1) * EMB], start=start, stop=stop)
                last.then_inc(chunk_used, 1)

            def run_block(g, b, par, hooks={}):
                gb = g * BLOCKS + b
                first = isinstance(b, int) and b == 0
                pe.wait_ge(cross_ready, gb + 1)
                pe.wait_ge(w7_loaded[par], w7_count(gb, par))
                for c in range(CHUNKS):
                    turn(gb, par, c)
                    if c == 0 and not first:
                        through_w7(gb * CHUNKS - 1, 1 - par, CHUNKS - 1, g)
                    elif c > 0:
                        through_w7(gb * CHUNKS + c - 1, par, c - 1, g, start=first and c == 1)
                    if c in hooks:
                        hooks[c]()

            def w7_count(gb, par):
                return 16 * ((gb - par) // 2 + 1) if isinstance(gb, int) else 8 * (gb - par) + 16

            def pooled_turned(g):
                pe.wait_ge(q_ready, GT * (g + 1))
                pe.wait_ge(act_step, steps.act)
                if g >= 2:
                    pe.wait_ge(out8_ready, g - 1)
                if g >= 3:
                    pe.wait_ge(y_ready, g - 2)
                bank = acc[g % 2]
                for t in range(GT):
                    for c in range(QCN):
                        dst = bank[0:QC, t, c * P:(c + 1) * P] if c < 4 else misc[0:QC, t * P:(t + 1) * P]
                        last = pe.transpose(dst, q[:, t, c * QC:(c + 1) * QC], ident[:])
                done(last)

            def make_h(g):
                after_copies(2)
                for t in range(GT):
                    dst = acc[g % 2][:, t, 0:EMB]
                    for c in range(QCN):
                        pe.matmul(dst, qt[:, t, c * P:(c + 1) * P], w5_sb[:, c, :],
                                  start=c == 0, stop=False)
                    last = pe.matmul(dst, ones, b5_sb, start=False, stop=True)
                done(last)

            def f7_turned(g):
                after_copies(1)
                for t in range(GT):
                    for c in range(ECN):
                        last = pe.transpose(acc[g % 2][0:EC, t, c * P:(c + 1) * P],
                                            f7s[:, t, c * EC:(c + 1) * EC], ident[:])
                done(last)

            def make_out8(g):
                after_copies(1)
                for t in range(GT):
                    dst = acc[g % 2][:, t, 0:EMB]
                    for c in range(ECN):
                        pe.matmul(dst, ht[:, t, c * P:(c + 1) * P], w68[:, c, :],
                                  start=c == 0, stop=False)
                        pe.matmul(dst, f7t[:, t, c * P:(c + 1) * P], w8_sb[:, c, :],
                                  start=False, stop=False)
                    last = pe.matmul(dst, ones, bias8, start=False, stop=True)
                done(last)

            def h_turned(g):
                pe.wait_ge(hh_ready, 2 * (g + 1))
                if g:
                    pe.wait_ge(out8_ready, g)
                bank = acc[(g + 1) % 2]
                for t in range(GT):
                    for c in range(ECN):
                        last = pe.transpose(bank[0:EC, t, c * P:(c + 1) * P],
                                            hh[:, t, c * EC:(c + 1) * EC], ident[:])
                done(last)
                steps.act += 1

            def z_turned(g):
                pe.wait_ge(rows_done, ROWS_AT[g + 2] if g + 2 <= GROUPS else ROWS_END)
                pe.wait_ge(act_step, steps.act)
                for c in range(ZCN):
                    for t in range(GT):
                        last = pe.transpose(misc[0:ZC, (c * GT + t) * P:(c * GT + t + 1) * P],
                                            z[:, g % 2, t, c * ZC:(c + 1) * ZC], ident[:])
                done(last)

            def make_h1(g):
                after_copies(1)
                pe.wait_ge(out8_ready, min(g + 2, GROUPS))
                for m in range(M1):
                    dst = acc[(g + 1) % 2][:, m // 2, m % 2 * GB:(m % 2 + 1) * GB]
                    for c in range(ZCN):
                        pe.matmul(dst, top1_sb[:, c, m * P:(m + 1) * P], zt[:, c, :],
                                  start=c == 0, stop=False)
                    last = pe.matmul(dst, top1c_sb[:, m * P:(m + 1) * P],
                                     ctx_sb[:, g * GB:(g + 1) * GB], start=False, stop=True)
                done(last)

            def make_h2(g):
                after_copies(M1)
                for m in range(M2):
                    for c in range(M1):
                        last = pe.matmul(misc[:, m * GB:(m + 1) * GB], top2_sb[:, c, m * P:(m + 1) * P],
                                         h1t[:, c, :], start=c == 0, stop=c == M1 - 1)
                done(last)

            def make_y(g):
                after_copies(M2)
                for c in range(M2):
                    last = pe.matmul(acc[(g + 1) % 2][0:1, 0, 0:GB], top3_sb[:, c:c + 1], h2t[:, c, :],
                                     start=c == 0, stop=c == M2 - 1)
                done(last)

            BURSTS = {"f7": f7_turned, "out8": make_out8, "ht": h_turned,
                      "zt": z_turned, "h1": make_h1, "h2": make_h2, "y": make_y}

            pe.wait_ge(score_consts, 32)
            for head in range(2):
                last = pe.matmul(acc[1][:, head, 0:EMB + 1], score_v[:, head, :], score_w[:, head, :],
                                 start=True, stop=True)
            done(last)
            steps.act += 1
            pe.wait_ge(consts, 16 * CONSTS)
            pe.wait_ge(filled, 2)
            for m in range(ECN):
                for c in range(ECN):
                    last = pe.matmul(turned[m][0:EC, 0:EMB], w6t[:, c, m * EC:(m + 1) * EC], w8a[:, c, :],
                                     start=c == 0, stop=c == ECN - 1)
            for c in range(ECN):
                pe.matmul(misc[0:1, 0:EMB], b67[:, c:c + 1], w8a[:, c, :], start=c == 0, stop=False)
                pe.matmul(misc[0:1, 0:EMB], b67[:, ECN + c:ECN + c + 1], w8_sb[:, c, :],
                          start=False, stop=False)
            done(pe.matmul(misc[0:1, 0:EMB], ones[:, 0:1], b8_sb, start=False, stop=True))
            steps.act += ECN + 1
            pooled_turned(0)
            make_h(0)
            for g in range(GROUPS):
                hooks = {}
                for i, (name, of) in enumerate(bursts_of(g)):
                    hooks[1 + 2 * i] = lambda name=name, of=of: BURSTS[name](of)
                for b in range(2):
                    run_block(g, b, b, {at - b * CHUNKS: hook for at, hook in hooks.items()
                                        if 0 <= at - b * CHUNKS < CHUNKS})
                with pe.Fori(1, BLOCKS // 2 - 1) as pair:
                    for par in range(2):
                        run_block(g, 2 * pair + par, par)
                more = g + 1 < GROUPS
                run_block(g, BLOCKS - 2, 0, {1: lambda: pooled_turned(g + 1),
                                             4: lambda: make_h(g + 1)} if more else {})
                run_block(g, BLOCKS - 1, 1)
                through_w7((g + 1) * BLOCKS * CHUNKS - 1, 1, CHUNKS - 1, g, stop=True)
            for name, of in bursts_of(GROUPS) + [(n, GROUPS - 1) for n in ("zt", "h1", "h2", "y")]:
                BURSTS[name](of)

        @block.scalar
        def _(act):
            steps = Steps()

            def copies(*made, wait=True):
                if wait:
                    steps.pe += 1
                    act.wait_ge(pe_step, steps.pe)
                for out, in_, func, kw in made:
                    act.activation(out, in_, func, **kw).then_inc(act_step, 1)
                    steps.act += 1

            def scale_chunk(b, c, gc):
                act.wait_ge(chunk_turned, CREDIT + gc + 1)
                if not (isinstance(gc, int) and gc < TR):
                    act.wait_ge(chunk_used, gc - TR + 1)
                act.activation(ct[0:CP, c % TR, :], turned[c % TR][0:CP, 0:GB], ACT.Copy,
                               scale=g_all[0:CP, bass.ds(b * CHUNKS + c, 1)]).then_inc(chunk_ready, 1)

            def run_block(g, b, hooks={}):
                for c in range(CHUNKS):
                    scale_chunk(b, c, (g * BLOCKS + b) * CHUNKS + c)
                    for hook in hooks.get(c, ()):
                        hook()

            def sum_abs(t, j):
                act.wait_ge(gathered[j], 16 * FG * (t + 1))
                for n in range(j * FG, (j + 1) * FG):
                    if FIELDS * t + n >= 2:
                        act.wait_ge(abs_done, FIELDS * t + n - 1)
                    act.activation(abs_junk[:, n % 2, :], x[:, n, :], ACT.Abs,
                                   accum_out=absum[:, n:n + 1]).then_inc(abs_done, 1)

            def abs_hooks(g, a, j):
                t = (g + 1) * GT + a
                rows = ROWS_AT[g] + a * per_tile(1, STAGE_LABELS[g]) + \
                    j * (DOTS + SLAB * STAGE_LABELS[g])

                def one(c):
                    if c == CHUNKS - FG:
                        act.wait_ge(rows_done, rows + 1)
                    n = c - (CHUNKS - FG)
                    act.wait_ge(abs_done, FIELDS * t + j * FG + n - 1)
                    at = bass.ds(j * FG + n, 1)
                    act.activation(abs_junk[:, n % 2, :], x[:, at, :].rearrange("p o e -> p (o e)"),
                                   ACT.Abs, accum_out=absum[:, at]).then_inc(abs_done, 1)
                return {c: lambda c=c: one(c) for c in range(CHUNKS - FG, CHUNKS)}

            def exp_scores(t, rows):
                act.wait_ge(rows_done, rows)
                for head in range(2):
                    act.activation(score[:, head, :], score[:, head, :], ACT.Exp,
                                   bias=score_u[:, head, EMB:EMB + 1]).then_inc(exp1_done, 1)

            def exp_softmax(t):
                act.wait_ge(ntop_ready, t + 1)
                for head in range(2):
                    act.activation(ex[:, head, :], score[:, head, :], ACT.Exp,
                                   bias=ntop[:, head:head + 1],
                                   accum_out=exsum[:, head:head + 1]).then_inc(exp2_done, 1)

            def after_pooled_turned(g):
                bank = acc[g % 2]
                copies((qt[:, :, 0:4 * P], bank[0:QC, :, 0:4 * P], ACT.Copy, {}),
                       (qt[:, :, 4 * P:5 * P], misc[0:QC, 0:GT * P].rearrange("p (t b) -> p t b", t=GT),
                        ACT.Copy, {}))

            def after_h(g):
                steps.pe += 1
                act.wait_ge(pe_step, steps.pe)
                if g:
                    act.wait_ge(cross_ready, g * BLOCKS)
                for half in range(2):
                    act.activation(hh[:, :, half * EMB:(half + 1) * EMB], acc[g % 2][:, :, 0:EMB],
                                   ACT.Copy).then_inc(hh_ready, 1)

            def before_f7_turned(g):
                act.wait_ge(chunk_used, (g + 1) * BLOCKS * CHUNKS)
                copies((f7s, acc[g % 2][:, :, 0:EMB], ACT.Copy, {}), wait=False)

            def after_f7_turned(g):
                copies((f7t, acc[g % 2][0:EC, :, 0:ECN * P], ACT.Copy, {}))

            def after_out8(g):
                act.wait_ge(rows_done, ROWS_AT[g + 1])
                steps.pe += 1
                act.wait_ge(pe_step, steps.pe)
                act.activation(out8[:], acc[g % 2][:, :, 0:EMB], ACT.Copy).then_inc(out8_ready, 1)

            def after_h_turned(g):
                copies((ht[:], acc[(g + 1) % 2][0:EC, :, 0:ECN * P], ACT.Copy, {}))

            def after_z_turned(g):
                copies((zt, misc[0:ZC, :].rearrange("p (c b) -> p c b", c=ZCN), ACT.Copy, {}))

            def after_h1(g):
                copies(*((h1t[:, m, :], acc[(g + 1) % 2][:, m // 2, m % 2 * GB:(m % 2 + 1) * GB],
                          ACT.Relu, dict(bias=bias1_sb[:, m:m + 1])) for m in range(M1)))

            def after_h2(g):
                copies(*((h2t[:, m, :], misc[:, m * GB:(m + 1) * GB], ACT.Relu,
                          dict(bias=bias2_sb[:, m:m + 1])) for m in range(M2)))

            def after_y(g):
                steps.pe += 1
                act.wait_ge(pe_step, steps.pe)
                if g:
                    act.wait_ge(y_stored, 16 * g)
                act.activation(y_sb, acc[(g + 1) % 2][0:1, 0, 0:GB], ACT.Copy).then_inc(y_ready, 1)
                act.wait_ge(y_ready, g + 1)
                act.dma_start(y_out[g * GB:(g + 1) * GB, :].rearrange("b o -> o b"),
                              y_sb).then_inc(y_stored, 16)

            AFTER = {"f7": after_f7_turned, "out8": after_out8, "ht": after_h_turned,
                     "zt": after_z_turned, "h1": after_h1, "h2": after_h2, "y": after_y}

            steps.pe += 1
            act.wait_ge(pe_step, steps.pe)
            act.activation(score_u[:], acc[1][:, :, 0:EMB + 1], ACT.Copy).then_inc(act_step, 1)
            steps.act += 1
            act.wait_ge(consts, 16 * CONSTS)
            copies(*((w68[:, m, :], turned[m][0:EC, 0:EMB], ACT.Copy, {}) for m in range(ECN)),
                   (bias8, misc[0:1, 0:EMB], ACT.Copy, {}))
            for t in range(GT):
                for j in range(NFG):
                    sum_abs(t, j)
                exp_scores(t, JUNK + (t + 1) * per_tile(1, 0))
                exp_softmax(t)
            after_pooled_turned(0)
            after_h(0)
            act.wait_ge(g_ready, 2)
            for g in range(GROUPS):
                hooks = {}
                for i, (name, of) in enumerate(bursts_of(g)):
                    hooks[2 + 2 * i] = lambda name=name, of=of: AFTER[name](of)
                if g:
                    before_f7_turned(g - 1)
                more = g + 1 < GROUPS
                for b in range(2):
                    here = {at - b * CHUNKS: [hook] for at, hook in hooks.items()
                            if 0 <= at - b * CHUNKS < CHUNKS}
                    for at, hook in (abs_hooks(g, 0, b) if more else {}).items():
                        here.setdefault(at, []).append(hook)
                    run_block(g, b, here)
                begin = 2
                for a in range(GT if more else 0):
                    t = (g + 1) * GT + a
                    if a:
                        with act.Fori(begin, a * TB) as b:
                            run_block(g, b)
                    with act.Fori(0 if a else begin, NFG) as j:
                        run_block(g, a * TB + j, {c: [h] for c, h in abs_hooks(g, a, j).items()})
                    rows = ROWS_AT[g] + a * per_tile(1, STAGE_LABELS[g]) + \
                        rows_through(NFG - 1, 1, STAGE_LABELS[g]) + DOTS
                    run_block(g, a * TB + NFG, {2: [lambda: exp_scores(t, rows)],
                                                6: [lambda: exp_softmax(t)]})
                    begin = a * TB + NFG + 1
                with act.Fori(begin, BLOCKS - 2) as b:
                    run_block(g, b)
                run_block(g, BLOCKS - 2, {2: [lambda: after_pooled_turned(g + 1)],
                                          8: [lambda: after_h(g + 1)]} if more else {})
                run_block(g, BLOCKS - 1)
            before_f7_turned(GROUPS - 1)
            for name, of in bursts_of(GROUPS) + [(n, GROUPS - 1) for n in ("zt", "h1", "h2", "y")]:
                AFTER[name](of)
            act.wait_ge(y_stored, 16 * GROUPS)


def pair_order():
    d, i = np.meshgrid(np.arange(1, DISTANCES + 1), np.arange(EMB), indexing="ij")
    j = (i + d) % EMB
    once = ~((d == DISTANCES) & (i >= EMB // 2))
    return np.minimum(i, j).ravel(), np.maximum(i, j).ravel(), once.ravel()


_OUT = ((BATCH, 1), "float32")


def kernel(**inputs):
    import concourse.bacc as _bacc
    from concourse.bass_utils import run_bass_kernel_spmd as _run

    a = {k: np.asarray(v) for k, v in inputs.items()}
    lo, hi, once = pair_order()
    row_of = lo * EMB - lo * (lo + 1) // 2 - lo - 1 + hi
    w7 = np.zeros((BLOCKS, P, CHUNKS, EMB), np.float32)
    rows = np.zeros((BLOCKS * CHUNKS * CP, EMB), np.float32)
    rows[once] = a["L0_rec_w7"][row_of[once]]
    w7[:, :CP] = rows.reshape(BLOCKS, CHUNKS, CP, EMB).transpose(0, 2, 1, 3)

    def pair_rows(idx):
        out = np.zeros((P, BLOCKS * CHUNKS, RANK), np.float32)
        out[:CP] = a["L0_rec_v"][idx].reshape(-1, CP, RANK).transpose(1, 0, 2)
        return out.reshape(P, -1)

    def split(w, rows):
        return w.reshape(-1, rows, w.shape[-1]).transpose(1, 0, 2)

    def columns(b, rows):
        return b.reshape(-1, rows).T

    w_score = np.stack([np.concatenate([a["L0_rec_w1"], a["L0_rec_b1"][None]]).T,
                        np.concatenate([a["L0_rec_w3"], a["L0_rec_b3"][None]]).T], 1)
    v_score = np.stack([np.repeat(a["L0_rec_w2"], P, 1), np.repeat(a["L0_rec_w4"], P, 1)], 1)
    arrays = {
        "ids": a["ids"], **{f"tbl_{n}": a[f"tbl_{n}"] for n in range(FIELDS)},
        "labels": a["r_label_embedding"], "ctx_t": a["dense_ctx"].T,
        "w_score": w_score, "v_score": v_score,
        "w5": split(a["L0_rec_w5"], QC), "b5": a["L0_rec_b5"][None],
        "w6t": split(a["L0_rec_w6"].T, EC),
        "b67": np.concatenate([columns(a["L0_rec_b6"], EC), columns(a["L0_rec_b7"], EC)], 1),
        "w7": w7.reshape(BLOCKS, P, -1),
        "w8": split(a["L0_rec_w8"], EC), "b8": a["L0_rec_b8"][None],
        "v_i": pair_rows(lo), "v_j": pair_rows(hi),
        "top1": split(a["W_top1"][:LABELS], ZC), "top1_ctx": a["W_top1"][LABELS:],
        "bias1": columns(a["b_top1"], P), "top2": split(a["W_top2"], P),
        "bias2": columns(a["b_top2"], P), "top3": columns(a["W_top3"], P),
        "ident": np.eye(P, dtype=np.float32),
    }
    nc = _bacc.Bacc("TRN2", target_bir_lowering=False, num_devices=1)
    sent, aps = {}, {}
    for name, array in arrays.items():
        array = np.ascontiguousarray(array)
        sent[f"in_{name}"] = array
        aps[name] = nc.dram_tensor(f"in_{name}", array.shape, mybir.dt.from_np(array.dtype),
                                   kind="ExternalInput").ap()
    shape, dtype = _OUT
    y = nc.dram_tensor("out_y", shape, mybir.dt.from_np(np.dtype(dtype)), kind="ExternalOutput").ap()
    g = aps
    dlrm_tower(nc, g["ids"], [g[f"tbl_{n}"] for n in range(FIELDS)], g["labels"], g["ctx_t"],
               g["w_score"], g["v_score"], g["w5"], g["b5"], g["w6t"], g["b67"], g["w7"],
               g["w8"], g["b8"], g["v_i"], g["v_j"], g["top1"], g["top1_ctx"], g["bias1"],
               g["top2"], g["bias2"], g["top3"], g["ident"], y)
    return _run(nc, [sent], core_ids=[0]).results[0]["out_y"]
```

```python
from contextlib import ExitStack

import numpy as np

import concourse.bass as bass
from concourse import mybir

F32 = mybir.dt.float32
I32 = mybir.dt.int32
ALU = mybir.AluOpType
ACT = mybir.ActivationFunctionType
AX_X = mybir.AxisListType.X

P = 128
BATCH, FIELDS, EMB, LABELS, RANK, HIDDEN = 1024, 50, 300, 200, 4, 8
CTX, TOP1, TOP2 = 16, 512, 256
TILES = BATCH // P
GT = 2
GROUPS = TILES // GT
GB = GT * P
PAD = float(-2 ** 32 + 1)

DISTANCES = EMB // 2
FINE = 5
COARSE = DISTANCES // FINE
PHASE_UNITS = [COARSE, COARSE, COARSE // 2]
PHASE_AT = [0, COARSE, 2 * COARSE]
REST = EMB - 2 * P
UNITS = sum(PHASE_UNITS)
CHUNKS = UNITS * FINE
TU = UNITS // GT
RING = 3
FG = 10
NFG = FIELDS // FG
SLAB = 8
SLABS = LABELS // SLAB
SLOTS = 3
JUNK = 4
QC, QCN = 120, 2 * EMB // 120
EC, ECN = 100, EMB // 100
ZC, ZCN = 100, LABELS // 100
M1, M2 = TOP1 // P, TOP2 // P

DOTS = 2 * FG
HALF = FG

QUOTA = [0, 21, 21, 33, SLABS]
LABEL_PLAN, _left = [], [(g, s) for g in range(GROUPS) for s in range(SLABS)]
for _stage, _n in enumerate(QUOTA):
    LABEL_PLAN.append(_left[:_n])
    _left = _left[_n:]
    assert all(group < _stage for group, _ in LABEL_PLAN[-1])
assert not _left
assert all(n % SLOTS == 0 for n in QUOTA[:-1])
STAGE_POOLS = [g < GROUPS - 1 for g in range(GROUPS)] + [False]


def order(stage):
    items = []
    slabs = iter([("slab", i) for i in range(QUOTA[stage])] or [("idle", i) for i in range(QUOTA[1])])

    def take(n):
        return [item for _, item in zip(range(n), slabs)]

    if STAGE_POOLS[stage]:
        for j in range(NFG):
            items += [("dots", 2 * j), ("dots", 2 * j + 1)] + take(1)
        items += take(3) + [("mask", 0)] + take(2) + [("normalise", 0)]
        for j in range(NFG):
            items += [("wsums", 2 * j), ("wsums", 2 * j + 1)] + take(1)
        items += [("pooled", 0)]
    return items + take(SLABS * GROUPS)


COST = {"dots": HALF, "wsums": HALF, "slab": SLAB, "idle": SLAB, "mask": 0, "normalise": 0, "pooled": 0}


def plan(stage):
    steps, spent = [[] for _ in range(TU)], 0
    total = sum(COST[kind] for kind, _ in order(stage))
    for kind, n in order(stage):
        steps[min(spent * TU // total, TU - 1)].append((kind, n))
        spent += COST[kind]
    return steps


PLANS = [plan(stage) for stage in range(GROUPS)]
WSUMS = 2 * FIELDS + 4
CHAIN = 7
CONSTS = 17
FINE_COPIES = (FINE + 1) // 2
CREDIT = RING


def pick(a, first, second):
    return first + a * (second - first)


def phase_of(u):
    return 0 if u < PHASE_AT[1] else 1 if u < PHASE_AT[2] else 2


def per_tile(stage):
    return NFG * DOTS * STAGE_POOLS[stage] + QUOTA[stage] * SLAB


def rows_before(stage, kind, n):
    items = order(stage)
    return sum(COST[k] for k, _ in items[:items.index((kind, n))] if k in ("dots", "slab"))


POOL_ROWS = NFG * DOTS
ROWS_AT = [JUNK + GT * POOL_ROWS]
LOADS_AT = [[0] * SLOTS]
for _stage in range(GROUPS + 1):
    ROWS_AT.append(ROWS_AT[-1] + GT * per_tile(_stage))
    LOADS_AT.append([n + GT * len(range(slot, QUOTA[_stage], SLOTS))
                     for slot, n in enumerate(LOADS_AT[-1])])


def slot_loads(stage, a, i):
    slot = i % SLOTS
    return LOADS_AT[stage][slot] + a * len(range(slot, QUOTA[stage], SLOTS)) + i // SLOTS + 1


def dlrm_tower(nc, ids, tables, labels, ctx_t, w_score, b_rep, w5, b5, w6, b67_in, w7, w8, b8,
               v_i, v_j, top1, top1_ctx, bias1, top2, bias2, top3, ident_in, y_out):
    with ExitStack() as ctx:
        def sb(name, shape, dt=F32):
            return ctx.enter_context(nc.sbuf_tensor(name, shape, dt))

        def ps(name, shape):
            return ctx.enter_context(nc.psum_tensor(name, shape, F32))

        def sem(name):
            return ctx.enter_context(nc.semaphore(name))

        ident = sb("ident", [P, P])
        w5_sb = sb("w5_sb", [QC, QCN, EMB])
        w68 = sb("w68", [EC, ECN, EMB])
        w8_sb = sb("w8_sb", [EC, ECN, EMB])
        top1_sb = sb("top1_sb", [ZC, ZCN, TOP1])
        bias1_sb = sb("bias1_sb", [P, M1])
        top2_sb = sb("top2_sb", [P, M1, TOP2])
        bias2_sb = sb("bias2_sb", [P, M2])
        top3_sb = sb("top3_sb", [P, M2])
        pads = sb("pads", [P, FIELDS])
        g_all = sb("g_all", [P, CHUNKS])
        score_u = sb("score_u", [P, 2, EMB + 1])
        narrow = sb("narrow", [48, BATCH + TOP1])
        b5_sb = narrow[0:1, 0:EMB]
        bias8 = narrow[0:1, EMB:2 * EMB]
        b8_sb = narrow[0:1, 2 * EMB:3 * EMB]
        y_sb = narrow[0:1, BATCH:BATCH + GB]
        ones = narrow[0:1, BATCH + GB:BATCH + GB + P]
        ctx_sb = narrow[32:32 + CTX, 0:BATCH]
        top1c_sb = narrow[32:32 + CTX, BATCH:BATCH + TOP1]
        ids_sb = sb("ids_sb", [P, FIELDS], I32)
        x = sb("x", [P, FIELDS, EMB])
        absum = sb("absum", [P, FIELDS])
        columns = sb("columns", [P, 6, 2])
        top, ntop, exsum, rsum, tick = (columns[:, i, :] for i in range(5))
        abs_junk = sb("abs_junk", [P, 2, EMB], mybir.dt.bfloat16)
        score = sb("score", [P, 2, FIELDS])
        empty = sb("empty", [P, FIELDS], I32)
        ex = sb("ex", [P, 2, FIELDS])
        qa = sb("qa", [P, 2, 2, EMB])
        q = sb("q", [P, GT, 2 * EMB])
        hh = sb("hh", [P, GT, 2 * EMB])
        fine = sb("fine", [P, 2, FINE, GB])
        picked = sb("picked", [P, RING, GT, P])
        prod = sb("prod", [P, RING, FINE, GB])
        w7_sb = sb("w7_sb", [P, RING, FINE * EMB])
        ht = sb("ht", [EC, GT, ECN * P])
        out8 = sb("out8", [P, 3, GT, EMB])
        spare = sb("spare", [P, GT * QCN * P])
        qflat = q[:].rearrange("p t n -> p (t n)")
        qt = spare[0:QC, :].rearrange("p (t n) -> p t n", t=GT)
        f7s = qflat[:, 0:GT * EMB].rearrange("p (t e) -> p t e", t=GT)
        f7t = spare[0:EC, 0:GT * ECN * P].rearrange("p (t n) -> p t n", t=GT)
        zt = qflat[0:ZC, 0:ZCN * GB].rearrange("p (c b) -> p c b", c=ZCN)
        h1t = spare[:, 0:M1 * GB].rearrange("p (c b) -> p c b", c=M1)
        h2t = qflat[:, 0:M2 * GB].rearrange("p (c b) -> p c b", c=M2)
        lab = sb("lab", [P, SLOTS, SLAB, EMB])
        start = lab[:].rearrange("p s k e -> p (s k e)")
        at = [0]

        def early(rows, *dims):
            n = int(np.prod(dims))
            view = start[0:rows, at[0]:at[0] + n]
            at[0] += n
            return view.rearrange("p (a b) -> p a b", a=dims[0]) if len(dims) == 2 else view

        score_w = early(HIDDEN, 2, EMB + 1)
        score_v = early(HIDDEN, 2, P)
        w6t = early(EC, ECN, EMB)
        w8a = early(EC, ECN, EMB)
        b67 = early(EC, 2 * ECN)
        junk = sb("junk", [P, JUNK, EMB])
        z = sb("z", [P, 3, GT, LABELS])

        acc = [ps(f"acc{i}", [P, GT, 512]) for i in range(2)]
        coarse = ps("coarse", [P, RING, 512])
        misc = ps("misc", [P, 512])

        score_consts = sem("score_consts")
        consts = sem("consts")
        filled = sem("filled")
        g_ready = sem("g_ready")
        ids_loaded = sem("ids_loaded")
        gathered = [sem(f"gathered{j}") for j in range(NFG)]
        abs_done = sem("abs_done")
        pool_ticks = sem("pool_ticks")
        rows_done = sem("rows_done")
        exp1_done = sem("exp1_done")
        chain = sem("chain")
        ntop_ready = sem("ntop_ready")
        exp2_done = sem("exp2_done")
        wsum_done = sem("wsum_done")
        q_ready = sem("q_ready")
        hh_ready = sem("hh_ready")
        cross_ready = sem("cross_ready")
        w7_loaded = [sem(f"w7_loaded{i}") for i in range(RING)]
        picked_ready = sem("picked_ready")
        coarse_ready = sem("coarse_ready")
        fine_ready = sem("fine_ready")
        chunk_ready = sem("chunk_ready")
        unit_used = sem("unit_used")
        pe_step = sem("pe_step")
        act_step = sem("act_step")
        out8_ready = sem("out8_ready")
        lab_loaded = [sem(f"lab_loaded{i}") for i in range(SLOTS)]
        y_ready = sem("y_ready")
        y_stored = sem("y_stored")

        v_rows = prod[:].rearrange("p r m b -> p (r m b)")[:, 0:2 * CHUNKS * RANK].rearrange(
            "p (two n) -> p two n", two=2)
        label_rows = labels.rearrange("(t p) k e -> t p (k e)", p=P)
        id_rows = ids.rearrange("(t p) n -> t p n", p=P)

        block = ctx.enter_context(nc.Block())

        @block.sync
        def _(sp):
            sp.dma_start(score_w, w_score).then_inc(score_consts, 16)
            sp.dma_start(score_v, b_rep).then_inc(score_consts, 16)
            sp.dma_start(v_rows[:, 0, :], v_i).then_inc(consts, 16)
            sp.dma_start(v_rows[:, 1, :], v_j).then_inc(consts, 16)
            for dst, src in ((ident[:], ident_in), (w5_sb[:], w5), (b5_sb, b5), (w6t, w6), (b67, b67_in),
                             (w8a, w8[:, 0:ECN, :]), (w8_sb[:], w8[:, ECN:2 * ECN, :]), (b8_sb, b8),
                             (top1_sb[:], top1), (top1c_sb, top1_ctx), (bias1_sb[:], bias1),
                             (top2_sb[:], top2), (bias2_sb[:], bias2), (top3_sb[:], top3),
                             (ctx_sb, ctx_t)):
                sp.dma_start(dst, src).then_inc(consts, 16)

            def load_w7(unit, u, slot):
                if not (isinstance(unit, int) and unit < RING):
                    sp.wait_ge(unit_used, CREDIT + unit - RING + 1)
                sp.dma_start(w7_sb[:, slot, :], w7[u]).then_inc(w7_loaded[slot], 16)

            def load_slab(stage, a, i):
                before = ROWS_AT[stage] + a * per_tile(stage)
                if i >= SLOTS:
                    used = before + rows_before(stage, "slab", i - SLOTS) + SLAB
                else:
                    used = before - (SLOTS - 1 - i) * SLAB if stage < GROUPS else before
                sp.wait_ge(rows_done, used)
                group, s = LABEL_PLAN[stage][i]
                sp.dma_start(lab[:, i % SLOTS, :, :].rearrange("p k e -> p (k e)"),
                             label_rows[group * GT + a, :, s * SLAB * EMB:(s + 1) * SLAB * EMB]
                             ).then_inc(lab_loaded[i % SLOTS], 16)

            for u in range(RING):
                load_w7(u, u, u)
            with sp.Fori(1, UNITS // RING) as n:
                for i in range(RING):
                    load_w7(n * RING + i, n * RING + i, i)
            for g in range(1, GROUPS):
                for u in range(UNITS):
                    load_w7(g * UNITS + u, u, u % RING)
                    a, step = divmod(u, TU)
                    for kind, i in PLANS[g][step] if a < GT else ():
                        if kind == "slab":
                            load_slab(g, a, i)
            with sp.Fori(0, GT) as a:
                for i in range(QUOTA[GROUPS]):
                    load_slab(GROUPS, a, i)

        @block.gpsimd
        def _(pool):
            def carry(tile_ticks, i):
                pool.wait_ge(pool_ticks, tile_ticks + i + 1)
                pool.tensor_tensor(tick[:, 1:2], tick[:, 0:1], tick[:, 0:1],
                                   ALU.add).then_inc(pool_ticks, 1)

            def tile(t, first=False):
                pool.dma_start(ids_sb[:], id_rows[t]).then_inc(ids_loaded, 16)
                pool.wait_ge(ids_loaded, 16 * (t + 1))
                carry(0 if first else t * (NFG + 1) - NFG, 0)
                for n in range(FIELDS):
                    j = n // FG
                    if n % FG == 0 and not first:
                        pool.wait_ge(wsum_done, WSUMS * t - 2 * FIELDS + 2 * FG * (j + 1))
                        carry(t * (NFG + 1) - NFG, j + 1)
                    pool.indirect_dma_start(
                        out=x[:, n, :], out_offset=None, in_=tables[n],
                        in_offset=bass.IndirectOffsetOnAxis(ap=ids_sb[:, n:n + 1], axis=0)
                    ).then_inc(gathered[j], 16)
                for j in range(NFG):
                    pool.wait_ge(gathered[j], 16 * FG * (t + 1))

            pool.memset(tick, 0.0).then_inc(pool_ticks, 1)
            tile(0, first=True)
            with pool.Fori(1, TILES) as t:
                tile(t)

        @block.vector
        def _(dve):
            dve.memset(ones, 1.0).then_inc(filled, 1)
            dve.memset(pads[:], PAD).then_inc(filled, 1)
            for r in range(JUNK):
                dve.memset(junk[:, r, :], 0.0).then_inc(rows_done, 1)
            dve.wait_ge(consts, 16 * CONSTS)
            dve.tensor_tensor(v_rows[:, 0, :], v_rows[:, 0, :], v_rows[:, 1, :],
                              ALU.mult).then_inc(g_ready, 1)
            dve.wait_ge(g_ready, 1)
            dve.tensor_reduce(g_all[:], v_rows[:, 0, :].rearrange("p (n r) -> p n r", r=RANK),
                              AX_X, ALU.add).then_inc(g_ready, 1)
            dve.wait_ge(g_ready, 2)
            dve.wait_ge(filled, 2)
            dve.wait_ge(act_step, 1)

            def row(count, i, in0, in1, out):
                dve.wait_ge(rows_done, count - JUNK + 1)
                dve.scalar_tensor_tensor(junk[:, i % JUNK, :], in0, 1.0, in1, ALU.mult, ALU.mult,
                                         accum_out=out).then_inc(rows_done, 1)

            def dots(t, count, half):
                if half % 2 == 0:
                    dve.wait_ge(gathered[half // 2], 16 * FG * (t + 1))
                for i in range(HALF):
                    n, head = (half * HALF + i) // 2, i % 2
                    row(count + i, half * HALF + i, x[:, n, :], score_u[:, head, 0:EMB],
                        score[:, head, n:n + 1])

            def then(t, k):
                dve.wait_ge(chain, t * CHAIN + k)

            def mask(t):
                dve.wait_ge(abs_done, FIELDS * (t + 1))
                dve.tensor_scalar(empty[:], absum[:], 0.0, None, ALU.is_equal).then_inc(chain, 1)
                dve.wait_ge(exp1_done, 2 * (t + 1))
                then(t, 1)
                dve.memset(qa[:], 0.0).then_inc(wsum_done, 4)
                for head in range(2):
                    dve.copy_predicated(score[:, head, :], empty[:], pads[:]).then_inc(chain, 1)
                then(t, 3)
                dve.tensor_reduce(top, score[:], AX_X, ALU.max).then_inc(chain, 1)
                then(t, 4)
                dve.tensor_scalar(ntop, top, -1.0, None, ALU.mult).then_inc(ntop_ready, 1)

            def normalise(t):
                dve.wait_ge(exp2_done, 2 * (t + 1))
                dve.reciprocal(rsum, exsum).then_inc(chain, 1)
                then(t, 5)
                for head in range(2):
                    dve.tensor_scalar(ex[:, head, :], ex[:, head, :], rsum[:, head:head + 1], None,
                                      ALU.mult).then_inc(chain, 1)
                then(t, 7)

            def wsums(t, half):
                for i in range(half * HALF, (half + 1) * HALF):
                    n, head = i // 2, i % 2
                    dve.wait_ge(wsum_done, WSUMS * t + i + 1)
                    part = qa[:, n % 2, head, :]
                    dve.scalar_tensor_tensor(part, x[:, n, :], ex[:, head, n:n + 1], part,
                                             ALU.mult, ALU.add).then_inc(wsum_done, 1)

            def pooled(t, a):
                dve.wait_ge(wsum_done, WSUMS * (t + 1))
                dve.tensor_tensor(q[:, a, :].rearrange("p (h e) -> p h e", h=2), qa[:, 0], qa[:, 1],
                                  ALU.add).then_inc(q_ready, 1)
                dve.wait_ge(q_ready, t + 1)

            def make_cross(g, a, i):
                here, there = i, TU + i
                unit = g * UNITS + a * TU + i
                slot = pick(a, here % RING, there % RING)
                phases = [phase_of(here), phase_of(min(there, UNITS - 1))]
                if here in PHASE_AT or there in PHASE_AT:
                    dve.wait_ge(fine_ready, FINE_COPIES * (4 * g + pick(a, *((1, 2, 4)[ph] for ph in phases))))
                dve.wait_ge(coarse_ready, unit + 1)
                dve.wait_ge(unit_used, CREDIT + unit - RING + 1)
                window = coarse[:, bass.ds(slot, 1), 0:GB]
                window = bass.AP(tensor=window.tensor, offset=window.offset,
                                 ap=[list(window.ap[0]), [0, FINE], [1, GB]])
                fines = fine[:, bass.ds(pick(a, *((3 * g + ph) % 2 for ph in phases)), 1), :, :]
                out = prod[:, bass.ds(slot, 1), :, :]
                dve.tensor_tensor(out.rearrange("p o m b -> p (o m) b"),
                                  fines.rearrange("p o m b -> p (o m) b"), window,
                                  ALU.mult).then_inc(cross_ready, 1)

            def slab(stage, a, i, count):
                group, s = LABEL_PLAN[stage][i]
                if i == 0 or LABEL_PLAN[stage][i - 1][0] != group:
                    dve.wait_ge(out8_ready, group + 1)
                dve.wait_ge(lab_loaded[i % SLOTS], 16 * slot_loads(stage, a, i))
                for k in range(SLAB):
                    row(count + k, k, lab[:, i % SLOTS, k, :], out8[:, group % 3, a, :],
                        z[:, group % 3, a, s * SLAB + k:s * SLAB + k + 1])

            def stage(g):
                make_cross(g, 0, 0)
                with dve.Fori(0, GT) as a:
                    before = ROWS_AT[g] + a * per_tile(g)
                    t = (g + 1) * GT + a
                    for step in range(TU):
                        make_cross(g, a, step + 1)
                        for kind, n in PLANS[g][step]:
                            if kind == "slab":
                                slab(g, a, n, before + rows_before(g, kind, n))
                            elif kind == "dots":
                                dots(t, before + rows_before(g, kind, n), n)
                            elif kind == "mask":
                                mask(t)
                            elif kind == "normalise":
                                normalise(t)
                            elif kind == "wsums":
                                wsums(t, n)
                            elif kind == "pooled":
                                pooled(t, a)

            with dve.Fori(0, GT) as a:
                for half in range(2 * NFG):
                    dots(a, JUNK + a * POOL_ROWS + half * HALF, half)
                mask(a)
                normalise(a)
                for half in range(2 * NFG):
                    wsums(a, half)
                pooled(a, a)
            dve.engine_nop().then_inc(unit_used, CREDIT)
            for g in range(GROUPS):
                stage(g)
            with dve.Fori(0, GT) as a:
                for i in range(QUOTA[GROUPS]):
                    slab(GROUPS, a, i, ROWS_AT[GROUPS] + a * per_tile(GROUPS) +
                         rows_before(GROUPS, "slab", i))

        class Steps:

            def __init__(self):
                self.pe = self.act = self.fine = 0

        def bursts_of(stage):
            names = []
            if stage >= 1:
                names += [("f7", stage - 1), ("out8", stage - 1)]
            if stage < GROUPS:
                names += [("ht", stage)]
            if stage == GROUPS:
                groups = range(GROUPS - 3, GROUPS)
            else:
                groups = range(stage - 3, stage - 2) if stage >= 3 else ()
            for g in groups:
                names += [(n, (g, stage)) for n in ("zt", "h1", "h2", "y")]
            return names

        AHEAD = 3
        FIRST_BURST, BURST_STEP = 2, AHEAD + 1
        LAST = UNITS - 5
        POOLED_AT = LAST * FINE
        H_AT = POOLED_AT + 5
        FIRST_FINE_AT = [H_AT + 4 + 4 * n for n in range(FINE_COPIES)]
        COARSE_AT = FIRST_FINE_AT[-1] + 4
        PICKS_AT = [H_AT + 3, H_AT + 7, H_AT + 12]
        HEAD = 6
        FINE_AT = {PHASE_AT[1] - 6: 1, PHASE_AT[2] - 6: 2}

        def plain(engine, run, u0, u1):
            whole = (u1 - u0) // RING
            if whole:
                with engine.Fori(0, whole) as n:
                    for i in range(RING):
                        run(u0 + n * RING + i, (u0 + i) % RING)
            for u in range(u0 + whole * RING, u1):
                run(u, u % RING)

        @block.tensor
        def _(pe):
            steps = Steps()

            def done(ins):
                ins.then_inc(pe_step, 1)
                steps.pe += 1

            def after_copies(n):
                steps.act += n
                pe.wait_ge(act_step, steps.act)

            def misc_free():
                pe.wait_ge(act_step, steps.act)
                if steps.fine:
                    pe.wait_ge(fine_ready, steps.fine)

            def turn_coarse(g, u, slot):
                unit = g * UNITS + u
                pe.wait_ge(picked_ready, unit + 1)
                if not (isinstance(unit, int) and unit < RING):
                    pe.wait_ge(cross_ready, unit - RING + 1)
                for t in range(GT):
                    last = pe.transpose(coarse[:, slot, t * P:(t + 1) * P], picked[:, slot, t, :],
                                        ident[:])
                last.then_inc(coarse_ready, 1)

            def turn_fine(phase, n):
                misc_free()
                for m in range(2 * n, min(2 * n + 2, FINE)):
                    for t in range(GT):
                        at = (m % 2 * GT + t) * P
                        if phase < 2:
                            start = (EMB, P)[phase] - m
                            last = pe.transpose(misc[:, at:at + P], hh[:, t, start:start + P],
                                                ident[:])
                        else:
                            start = 2 * P - m
                            last = pe.transpose(misc[0:P // 2, at:at + P],
                                                hh[:, t, start:start + P // 2], ident[:])
                done(last)
                steps.fine += 2 if phase == 2 else 1

            def run_unit(g, u, slot, hooks={}, first=False, last_unit=False):
                unit = g * UNITS + u
                pe.wait_ge(w7_loaded[slot], w7_count(unit, slot))
                for m in range(FINE):
                    pe.wait_ge(chunk_ready, unit * FINE + m + 1)
                    for t in range(GT):
                        last = pe.matmul(acc[g % 2][:, t, 0:EMB], prod[:, slot, m, t * P:(t + 1) * P],
                                         w7_sb[:, slot, m * EMB:(m + 1) * EMB],
                                         start=first and m == 0, stop=last_unit and m == FINE - 1)
                    if m == FINE - 1:
                        last.then_inc(unit_used, 1)
                    if m == 0 and not (isinstance(u, int) and u + 2 >= UNITS):
                        turn_coarse(g, u + 2, (slot + 2) % RING)
                    for hook in hooks.get(m, ()):
                        hook()

            def run(g, u0, u1, hooks={}):
                for u in range(u0, u1):
                    run_unit(g, u, u % RING, {m: hooks[u, m] for m in range(FINE) if (u, m) in hooks},
                             first=u == 0, last_unit=u == UNITS - 1)

            def w7_count(unit, slot):
                return 16 * ((unit - slot) // RING + 1)

            def pooled_turned(g):
                pe.wait_ge(q_ready, GT * (g + 1))
                misc_free()
                if g >= 2:
                    pe.wait_ge(out8_ready, g - 1)
                bank = acc[g % 2]
                for t in range(GT):
                    for c in range(QCN):
                        dst = bank[0:QC, t, c * P:(c + 1) * P] if c < 4 else misc[0:QC, t * P:(t + 1) * P]
                        last = pe.transpose(dst, q[:, t, c * QC:(c + 1) * QC], ident[:])
                done(last)

            def make_h(g):
                after_copies(2)
                for t in range(GT):
                    dst = acc[g % 2][:, t, 0:EMB]
                    for c in range(QCN):
                        pe.matmul(dst, qt[:, t, c * P:(c + 1) * P], w5_sb[:, c, :],
                                  start=c == 0, stop=False)
                    last = pe.matmul(dst, ones, b5_sb, start=False, stop=True)
                done(last)

            def f7_turned(g):
                after_copies(1)
                for t in range(GT):
                    for c in range(ECN):
                        last = pe.transpose(acc[g % 2][0:EC, t, c * P:(c + 1) * P],
                                            f7s[:, t, c * EC:(c + 1) * EC], ident[:])
                done(last)

            def make_out8(g):
                after_copies(1)
                for t in range(GT):
                    dst = acc[g % 2][:, t, 0:EMB]
                    for c in range(ECN):
                        pe.matmul(dst, ht[:, t, c * P:(c + 1) * P], w68[:, c, :],
                                  start=c == 0, stop=False)
                        pe.matmul(dst, f7t[:, t, c * P:(c + 1) * P], w8_sb[:, c, :],
                                  start=False, stop=False)
                    last = pe.matmul(dst, ones, bias8, start=False, stop=True)
                done(last)

            def h_turned(g):
                pe.wait_ge(hh_ready, 2 * (g + 1))
                if g:
                    pe.wait_ge(out8_ready, g)
                bank = acc[(g + 1) % 2]
                for t in range(GT):
                    for c in range(ECN):
                        last = pe.transpose(bank[0:EC, t, c * P:(c + 1) * P],
                                            hh[:, t, c * EC:(c + 1) * EC], ident[:])
                done(last)
                steps.act += 1

            def z_turned(at):
                g, stage = at
                last = max(i for i, slabs in enumerate(LABEL_PLAN) if g in (of for of, _ in slabs))
                pe.wait_ge(rows_done, ROWS_AT[last + 1])
                misc_free()
                for c in range(ZCN):
                    for t in range(GT):
                        last = pe.transpose(misc[0:ZC, (c * GT + t) * P:(c * GT + t + 1) * P],
                                            z[:, g % 3, t, c * ZC:(c + 1) * ZC], ident[:])
                done(last)

            def make_h1(at):
                g, stage = at
                """the first top layer over [z, context], turned"""
                after_copies(1)
                pe.wait_ge(out8_ready, stage)
                if g:
                    pe.wait_ge(y_ready, g)
                for m in range(M1):
                    dst = acc[(stage + 1) % 2][:, m // 2, m % 2 * GB:(m % 2 + 1) * GB]
                    for c in range(ZCN):
                        pe.matmul(dst, top1_sb[:, c, m * P:(m + 1) * P], zt[:, c, :],
                                  start=c == 0, stop=False)
                    last = pe.matmul(dst, top1c_sb[:, m * P:(m + 1) * P],
                                     ctx_sb[:, g * GB:(g + 1) * GB], start=False, stop=True)
                done(last)

            def make_h2(at):
                after_copies(M1)
                for m in range(M2):
                    for c in range(M1):
                        last = pe.matmul(misc[:, m * GB:(m + 1) * GB], top2_sb[:, c, m * P:(m + 1) * P],
                                         h1t[:, c, :], start=c == 0, stop=c == M1 - 1)
                done(last)

            def make_y(at):
                g, stage = at
                after_copies(M2)
                for c in range(M2):
                    last = pe.matmul(acc[(stage + 1) % 2][0:1, 0, 0:GB], top3_sb[:, c:c + 1], h2t[:, c, :],
                                     start=c == 0, stop=c == M2 - 1)
                done(last)

            BURSTS = {"f7": f7_turned, "out8": make_out8, "ht": h_turned,
                      "zt": z_turned, "h1": make_h1, "h2": make_h2, "y": make_y}

            pe.wait_ge(score_consts, 32)
            for head in range(2):
                last = pe.matmul(acc[1][:, head, 0:EMB + 1], score_v[:, head, :], score_w[:, head, :],
                                 start=True, stop=True)
            done(last)
            steps.act += 1
            pe.wait_ge(consts, 16 * CONSTS)
            pe.wait_ge(filled, 2)
            for m in range(ECN):
                for c in range(ECN):
                    last = pe.matmul(coarse[0:EC, m, 0:EMB], w6t[:, c, m * EC:(m + 1) * EC], w8a[:, c, :],
                                     start=c == 0, stop=c == ECN - 1)
            for c in range(ECN):
                pe.matmul(misc[0:1, 0:EMB], b67[:, c:c + 1], w8a[:, c, :], start=c == 0, stop=False)
                pe.matmul(misc[0:1, 0:EMB], b67[:, ECN + c:ECN + c + 1], w8_sb[:, c, :],
                          start=False, stop=False)
            done(pe.matmul(misc[0:1, 0:EMB], ones[:, 0:1], b8_sb, start=False, stop=True))
            steps.act += ECN + 1
            pooled_turned(0)
            make_h(0)

            def turn_first(g):
                pe.wait_ge(hh_ready, 2 * (g + 1))
                for n in range(FINE_COPIES):
                    turn_fine(0, n)
                first_coarse(g)

            def first_coarse(g):
                for u in range(2):
                    turn_coarse(g, u, u)

            turn_first(0)
            for g in range(GROUPS):
                hooks = {}
                for i, (name, of) in enumerate(bursts_of(g)):
                    hooks[divmod(FIRST_BURST + BURST_STEP * i, FINE)] = [
                        lambda name=name, of=of: BURSTS[name](of)]
                for at, phase in FINE_AT.items():
                    for n in range(FINE_COPIES):
                        hooks[at + n, 1] = [lambda phase=phase, n=n: turn_fine(phase, n)]
                if g + 1 < GROUPS:
                    hooks[divmod(POOLED_AT, FINE)] = [lambda: pooled_turned(g + 1)]
                    hooks[divmod(H_AT, FINE)] = [lambda: make_h(g + 1)]
                    for n in range(FINE_COPIES):
                        hooks[divmod(FIRST_FINE_AT[n], FINE)] = [lambda n=n: (
                            n == 0 and pe.wait_ge(hh_ready, 2 * (g + 2)), turn_fine(0, n))]
                    hooks[divmod(COARSE_AT, FINE)] = [lambda: first_coarse(g + 1)]
                one = lambda u, slot: run_unit(g, u, slot)
                run(g, 0, HEAD, hooks)
                plain(pe, one, HEAD, PHASE_AT[1] - 6)
                run(g, PHASE_AT[1] - 6, PHASE_AT[1] - 3, hooks)
                plain(pe, one, PHASE_AT[1] - 3, PHASE_AT[2] - 6)
                run(g, PHASE_AT[2] - 6, PHASE_AT[2] - 3, hooks)
                plain(pe, one, PHASE_AT[2] - 3, LAST)
                run(g, LAST, UNITS, hooks)
            for name, of in bursts_of(GROUPS):
                BURSTS[name](of)

        @block.scalar
        def _(act):
            steps = Steps()

            def copies(*made, wait=True):
                if wait:
                    steps.pe += 1
                    act.wait_ge(pe_step, steps.pe)
                for out, in_, func, kw in made:
                    act.activation(out, in_, func, **kw).then_inc(act_step, 1)
                    steps.act += 1

            def run_unit(g, u, slot, hooks={}):
                unit = g * UNITS + u
                act.wait_ge(cross_ready, unit + 1)
                if not (isinstance(u, int) and u + RING >= UNITS):
                    pick_window(g, u + RING, phase_now[0], slot)
                for m in range(FINE):
                    act.activation(prod[:, slot, m, :], prod[:, slot, m, :], ACT.Copy,
                                   scale=g_all[:, bass.ds(u * FINE + m, 1)]).then_inc(chunk_ready, 1)
                    for hook in hooks.get(m, ()):
                        hook()

            phase_now = [0]

            def pick_window(g, u, phase, slot):
                if not (isinstance(g, int) and isinstance(u, int) and g * UNITS + u < RING):
                    act.wait_ge(coarse_ready, g * UNITS + u - RING + 1)
                k = u - PHASE_AT[phase]
                if phase < 2:
                    cols = hh[:, :, bass.ds(P * phase + FINE * k + 1, P)]
                    out = picked[:, slot, :, :]
                else:
                    cols = hh[:, :, bass.ds(2 * P + 2 * FINE * k + 1, P // 2)]
                    cols = bass.AP(tensor=cols.tensor, offset=cols.offset,
                                   ap=[list(cols.ap[0]), list(cols.ap[1]), [FINE, 2], [1, P // 2]])
                    out = picked[:, slot, :, :].rearrange("p t (two n) -> p t two n", two=2)
                act.activation(out, cols, ACT.Copy).then_inc(picked_ready, 1)

            def run(g, u0, u1, hooks={}):
                for u in range(u0, u1):
                    phase_now[0] = phase_of(min(u + RING, UNITS - 1))
                    run_unit(g, u, u % RING, {m: hooks[u, m] for m in range(FINE) if (u, m) in hooks})

            def sum_abs(t, j):
                act.wait_ge(gathered[j], 16 * FG * (t + 1))
                for n in range(j * FG, (j + 1) * FG):
                    if FIELDS * t + n >= 2:
                        act.wait_ge(abs_done, FIELDS * t + n - 1)
                    act.activation(abs_junk[:, n % 2, :], x[:, n, :], ACT.Abs,
                                   accum_out=absum[:, n:n + 1]).then_inc(abs_done, 1)

            def abs_hooks(g, a, j):
                t = (g + 1) * GT + a
                rows = ROWS_AT[g] + a * per_tile(g) + j * rows_before(g, "dots", 2)

                def one(n):
                    if n == 0:
                        act.wait_ge(rows_done, rows + 1)
                    act.wait_ge(abs_done, FIELDS * t + j * FG + n - 1)
                    at = bass.ds(j * FG + n, 1)
                    act.activation(abs_junk[:, n % 2, :], x[:, at, :].rearrange("p o e -> p (o e)"),
                                   ACT.Abs, accum_out=absum[:, at]).then_inc(abs_done, 1)
                return {divmod(3 * FINE - FG + n, FINE): lambda n=n: one(n) for n in range(FG)}

            def abs_loop(g, a, j0):
                with act.Fori(j0, NFG) as j:
                    hooks = abs_hooks(g, a, j)
                    for i in range(3):
                        run_unit(g, a * TU + 3 * j + i, (a * TU + i) % RING,
                                 {m: [hooks[i, m]] for m in range(FINE) if (i, m) in hooks})

            def exp_scores(t, rows):
                act.wait_ge(rows_done, rows)
                for head in range(2):
                    act.activation(score[:, head, :], score[:, head, :], ACT.Exp,
                                   bias=score_u[:, head, EMB:EMB + 1]).then_inc(exp1_done, 1)

            def exp_softmax(t):
                act.wait_ge(ntop_ready, t + 1)
                for head in range(2):
                    act.activation(ex[:, head, :], score[:, head, :], ACT.Exp,
                                   bias=ntop[:, head:head + 1],
                                   accum_out=exsum[:, head:head + 1]).then_inc(exp2_done, 1)

            def after_pooled_turned(g):
                bank = acc[g % 2]
                copies((qt[:, :, 0:4 * P], bank[0:QC, :, 0:4 * P], ACT.Copy, {}),
                       (qt[:, :, 4 * P:5 * P], misc[0:QC, 0:GT * P].rearrange("p (t b) -> p t b", t=GT),
                        ACT.Copy, {}))

            def after_h(g):
                steps.pe += 1
                act.wait_ge(pe_step, steps.pe)
                if g:
                    act.wait_ge(picked_ready, g * UNITS)
                for half in range(2):
                    act.activation(hh[:, :, half * EMB:(half + 1) * EMB], acc[g % 2][:, :, 0:EMB],
                                   ACT.Copy).then_inc(hh_ready, 1)
                act.wait_ge(hh_ready, 2 * (g + 1))

            def before_f7_turned(g):
                act.wait_ge(unit_used, CREDIT + (g + 1) * UNITS)
                copies((f7s, acc[g % 2][:, :, 0:EMB], ACT.Copy, {}), wait=False)

            def after_f7_turned(g):
                copies((f7t, acc[g % 2][0:EC, :, 0:ECN * P], ACT.Copy, {}))

            def after_out8(g):
                if g >= 3:
                    act.wait_ge(rows_done, ROWS_AT[g])
                steps.pe += 1
                act.wait_ge(pe_step, steps.pe)
                act.activation(out8[:, g % 3], acc[g % 2][:, :, 0:EMB], ACT.Copy).then_inc(out8_ready, 1)

            def after_h_turned(g):
                copies((ht[:], acc[(g + 1) % 2][0:EC, :, 0:ECN * P], ACT.Copy, {}))

            def after_z_turned(at):
                copies((zt, misc[0:ZC, :].rearrange("p (c b) -> p c b", c=ZCN), ACT.Copy, {}))

            def after_h1(at):
                g, stage = at
                copies(*((h1t[:, m, :], acc[(stage + 1) % 2][:, m // 2, m % 2 * GB:(m % 2 + 1) * GB],
                          ACT.Relu, dict(bias=bias1_sb[:, m:m + 1])) for m in range(M1)))

            def after_h2(at):
                copies(*((h2t[:, m, :], misc[:, m * GB:(m + 1) * GB], ACT.Relu,
                          dict(bias=bias2_sb[:, m:m + 1])) for m in range(M2)))

            def after_y(at):
                g, stage = at
                steps.pe += 1
                act.wait_ge(pe_step, steps.pe)
                if g:
                    act.wait_ge(y_stored, 16 * g)
                act.activation(y_sb, acc[(stage + 1) % 2][0:1, 0, 0:GB], ACT.Copy).then_inc(y_ready, 1)
                act.wait_ge(y_ready, g + 1)
                act.dma_start(y_out[g * GB:(g + 1) * GB, :].rearrange("b o -> o b"),
                              y_sb).then_inc(y_stored, 16)

            AFTER = {"f7": after_f7_turned, "out8": after_out8, "ht": after_h_turned,
                     "zt": after_z_turned, "h1": after_h1, "h2": after_h2, "y": after_y}

            steps.pe += 1
            act.wait_ge(pe_step, steps.pe)
            act.activation(score_u[:], acc[1][:, :, 0:EMB + 1], ACT.Copy).then_inc(act_step, 1)
            steps.act += 1
            act.wait_ge(consts, 16 * CONSTS)
            copies(*((w68[:, m, :], coarse[0:EC, m, 0:EMB], ACT.Copy, {}) for m in range(ECN)),
                   (bias8, misc[0:1, 0:EMB], ACT.Copy, {}))
            for t in range(GT):
                for j in range(NFG):
                    sum_abs(t, j)
                exp_scores(t, JUNK + (t + 1) * POOL_ROWS)
                exp_softmax(t)
            def copy_fine(g, phase, n):
                steps.pe += 1
                act.wait_ge(pe_step, steps.pe)
                ms = range(2 * n, min(2 * n + 2, FINE))
                rows = P // 2 if phase == 2 else P
                for to in range(0, P, rows):
                    act.activation(fine[to:to + rows, (3 * g + phase) % 2, ms[0]:ms[-1] + 1, :],
                                   misc[0:rows, 0:len(ms) * GB].rearrange("p (m b) -> p m b", b=GB),
                                   ACT.Copy).then_inc(fine_ready, 1)

            after_pooled_turned(0)
            after_h(0)
            for u in range(RING):
                pick_window(0, u, 0, u)
            for n in range(FINE_COPIES):
                copy_fine(0, 0, n)
            act.wait_ge(g_ready, 2)
            for g in range(GROUPS):
                more = g + 1 < GROUPS
                hooks = {}
                for i, (name, of) in enumerate(bursts_of(g)):
                    hooks[divmod(FIRST_BURST + BURST_STEP * i + AHEAD, FINE)] = [
                        lambda name=name, of=of: AFTER[name](of)]
                for at, phase in FINE_AT.items():
                    for n in range(FINE_COPIES):
                        hooks[at + n, 4] = [lambda phase=phase, n=n: copy_fine(g, phase, n)]
                if g:
                    hooks[0, FIRST_BURST - 1] = [lambda: before_f7_turned(g - 1)]
                if more:
                    for j in range(HEAD // 3):
                        for (i, m), hook in abs_hooks(g, 0, j).items():
                            hooks.setdefault((3 * j + i, m), []).append(hook)
                    for a in range(GT):
                        rows = ROWS_AT[g] + a * per_tile(g) + \
                            rows_before(g, "dots", 2 * NFG - 1) + HALF
                        t = (g + 1) * GT + a
                        hooks[a * TU + 3 * NFG, 0] = [lambda t=t, rows=rows: exp_scores(t, rows)]
                        hooks[a * TU + 3 * NFG + 1, 0] = [lambda t=t: exp_softmax(t)]
                    hooks[divmod(POOLED_AT + AHEAD, FINE)] = [lambda: after_pooled_turned(g + 1)]
                    hooks[divmod(H_AT + 2, FINE)] = [lambda: after_h(g + 1)]
                    for u in range(RING):
                        hooks.setdefault(divmod(PICKS_AT[u], FINE), []).append(
                            lambda u=u: pick_window(g + 1, u, 0, u))
                    for n in range(FINE_COPIES):
                        hooks.setdefault(divmod(FIRST_FINE_AT[n] + 2, FINE), []).append(
                            lambda n=n: copy_fine(g + 1, 0, n))
                run(g, 0, HEAD, hooks)
                one = lambda u, slot: run_unit(g, u, slot)
                if more:
                    abs_loop(g, 0, HEAD // 3)
                    run(g, 3 * NFG, 3 * NFG + 2, hooks)
                    plain(act, one, 3 * NFG + 2, PHASE_AT[1] - 6)
                    run(g, PHASE_AT[1] - 6, PHASE_AT[1] - 3, hooks)
                    phase_now[0] = 1
                    plain(act, one, PHASE_AT[1] - 3, TU)
                    abs_loop(g, 1, 0)
                    run(g, TU + 3 * NFG, PHASE_AT[2] - 3, hooks)
                else:
                    plain(act, one, HEAD, PHASE_AT[1] - 6)
                    run(g, PHASE_AT[1] - 6, PHASE_AT[1] - 3, hooks)
                    phase_now[0] = 1
                    plain(act, one, PHASE_AT[1] - 3, PHASE_AT[2] - 6)
                    run(g, PHASE_AT[2] - 6, PHASE_AT[2] - 3, hooks)
                phase_now[0] = 2
                plain(act, one, PHASE_AT[2] - 3, LAST)
                run(g, LAST, UNITS, hooks)
            before_f7_turned(GROUPS - 1)
            for name, of in bursts_of(GROUPS):
                AFTER[name](of)
            act.wait_ge(y_stored, 16 * GROUPS)


def pair_order():
    u, m, p = np.meshgrid(np.arange(UNITS), np.arange(FINE), np.arange(P), indexing="ij")
    rest = u >= PHASE_AT[2]
    k = np.where(rest, 2 * (u - PHASE_AT[2]) + p // (P // 2), u % COARSE)
    d = FINE * k + m + 1
    p_in = np.where(rest, p % (P // 2), p)
    i = (np.where(rest, 2 * P, u // COARSE * P) - m + p_in) % EMB
    j = (i + d) % EMB
    lo, hi = np.minimum(i, j), np.maximum(i, j)
    once = ~(rest & (p_in >= REST)) & ~((d == DISTANCES) & (i >= DISTANCES))
    return lo, hi, once


_OUT = ((BATCH, 1), "float32")


def kernel(**inputs):
    import concourse.bacc as _bacc
    from concourse.bass_utils import run_bass_kernel_spmd as _run

    a = {k: np.asarray(v) for k, v in inputs.items()}
    lo, hi, once = pair_order()
    row_of = lo * EMB - lo * (lo + 1) // 2 - lo - 1 + hi
    w7 = np.zeros((UNITS, FINE, P, EMB), np.float32)
    w7[once] = a["L0_rec_w7"][row_of[once]]
    w7 = w7.transpose(0, 2, 1, 3)

    def pair_rows(idx):
        out = np.zeros((UNITS, FINE, P, RANK), np.float32)
        out[once] = a["L0_rec_v"][idx[once]]
        return out.transpose(2, 0, 1, 3).reshape(P, -1)

    def split(w, rows):
        return w.reshape(-1, rows, w.shape[-1]).transpose(1, 0, 2)

    def columns(b, rows):
        return b.reshape(-1, rows).T

    w_score = np.stack([np.concatenate([a["L0_rec_w1"], a["L0_rec_b1"][None]]).T,
                        np.concatenate([a["L0_rec_w3"], a["L0_rec_b3"][None]]).T], 1)
    v_score = np.stack([np.repeat(a["L0_rec_w2"], P, 1), np.repeat(a["L0_rec_w4"], P, 1)], 1)
    arrays = {
        "ids": a["ids"], **{f"tbl_{n}": a[f"tbl_{n}"] for n in range(FIELDS)},
        "labels": a["r_label_embedding"], "ctx_t": a["dense_ctx"].T,
        "w_score": w_score, "v_score": v_score,
        "w5": split(a["L0_rec_w5"], QC), "b5": a["L0_rec_b5"][None],
        "w6t": split(a["L0_rec_w6"].T, EC),
        "b67": np.concatenate([columns(a["L0_rec_b6"], EC), columns(a["L0_rec_b7"], EC)], 1),
        "w7": w7.reshape(UNITS, P, -1),
        "w8": split(a["L0_rec_w8"], EC), "b8": a["L0_rec_b8"][None],
        "v_i": pair_rows(lo), "v_j": pair_rows(hi),
        "top1": split(a["W_top1"][:LABELS], ZC), "top1_ctx": a["W_top1"][LABELS:],
        "bias1": columns(a["b_top1"], P), "top2": split(a["W_top2"], P),
        "bias2": columns(a["b_top2"], P), "top3": columns(a["W_top3"], P),
        "ident": np.eye(P, dtype=np.float32),
    }
    nc = _bacc.Bacc("TRN2", target_bir_lowering=False, num_devices=1)
    sent, aps = {}, {}
    for name, array in arrays.items():
        array = np.ascontiguousarray(array)
        sent[f"in_{name}"] = array
        aps[name] = nc.dram_tensor(f"in_{name}", array.shape, mybir.dt.from_np(array.dtype),
                                   kind="ExternalInput").ap()
    shape, dtype = _OUT
    y = nc.dram_tensor("out_y", shape, mybir.dt.from_np(np.dtype(dtype)), kind="ExternalOutput").ap()
    g = aps
    dlrm_tower(nc, g["ids"], [g[f"tbl_{n}"] for n in range(FIELDS)], g["labels"], g["ctx_t"],
               g["w_score"], g["v_score"], g["w5"], g["b5"], g["w6t"], g["b67"], g["w7"],
               g["w8"], g["b8"], g["v_i"], g["v_j"], g["top1"], g["top1_ctx"], g["bias1"],
               g["top2"], g["bias2"], g["top3"], g["ident"], y)
    return _run(nc, [sent], core_ids=[0]).results[0]["out_y"]
```

```python
from contextlib import ExitStack

import numpy as np

import concourse.bass as bass
from concourse import mybir

F32 = mybir.dt.float32
I32 = mybir.dt.int32
ALU = mybir.AluOpType
ACT = mybir.ActivationFunctionType
AX_X = mybir.AxisListType.X

P = 128
BATCH, FIELDS, EMB, LABELS, RANK, HIDDEN = 1024, 50, 300, 200, 4, 8
CTX, TOP1, TOP2 = 16, 512, 256
TILES = BATCH // P
GT = 2
GROUPS = TILES // GT
GB = GT * P
PAD = float(-2 ** 32 + 1)

DISTANCES = EMB // 2
FINE = 5
COARSE = DISTANCES // FINE
THIRD = P // 3
LEFT = EMB - 2 * P - THIRD
PHASE_UNITS = [COARSE, COARSE, 1, COARSE // 3]
PHASE_AT = [0, COARSE, 2 * COARSE, 2 * COARSE + 1]
PHASE_ROWS = [P, P, COARSE * LEFT, 3 * THIRD]
UNITS = sum(PHASE_UNITS)
CHUNKS = UNITS * FINE
TU = UNITS // GT
RING = 3
FG = 10
NFG = FIELDS // FG
SLAB = 8
SLABS = LABELS // SLAB
SLOTS = 3
DIAGS = 5
assert FIELDS % DIAGS == 0
END_SLOTS = 5
JUNK = 4
QC, QCN = 120, 2 * EMB // 120
EC, ECN = 100, EMB // 100
ZC, ZCN = 100, LABELS // 100
M1, M2 = TOP1 // P, TOP2 // P

DOTS = 2 * FG
HALF = FG

QUOTA = [0, 21, 21, 33, SLABS]
LABEL_PLAN, _left = [], [(g, s) for g in range(GROUPS) for s in range(SLABS)]
for _stage, _n in enumerate(QUOTA):
    LABEL_PLAN.append(_left[:_n])
    _left = _left[_n:]
    assert all(group < _stage for group, _ in LABEL_PLAN[-1])
assert not _left
assert all(n % SLOTS == 0 for n in QUOTA[:-1]) and QUOTA[-1] % END_SLOTS == 0
STAGE_POOLS = [g < GROUPS - 1 for g in range(GROUPS)] + [False]


def order(stage):
    items = []
    slabs = iter([("slab", i) for i in range(QUOTA[stage])] or [("idle", i) for i in range(QUOTA[1])])

    def take(n):
        return [item for _, item in zip(range(n), slabs)]

    if STAGE_POOLS[stage]:
        for j in range(NFG):
            items += [("dots", 2 * j), ("dots", 2 * j + 1)] + take(1)
        items += take(2) + [("mask", 0)] + take(3) + [("normalise", 0)]
        for j in range(NFG):
            items += [("wsums", 2 * j), ("wsums", 2 * j + 1)] + take(1)
        items += [("pooled", 0)]
    return items + take(SLABS * GROUPS)


COST = {"dots": HALF, "wsums": HALF, "slab": SLAB, "idle": SLAB, "mask": 0, "normalise": 0, "pooled": 0}


def plan(stage):
    steps, spent = [[] for _ in range(TU)], 0
    total = sum(COST[kind] for kind, _ in order(stage))
    for kind, n in order(stage):
        steps[min(spent * TU // total, TU - 1)].append((kind, n))
        spent += COST[kind]
    return steps


PLANS = [plan(stage) for stage in range(GROUPS)]
WSUMS = 2 * FIELDS
CHAIN = 8
CONSTS = 17
FINE_COPIES = (FINE + 1) // 2
CREDIT = RING


def pick(a, first, second):
    return first + a * (second - first)


def phase_of(u):
    return sum(u >= at for at in PHASE_AT) - 1


def per_tile(stage):
    return NFG * DOTS * STAGE_POOLS[stage] + QUOTA[stage] * SLAB


def rows_before(stage, kind, n):
    items = order(stage)
    return sum(COST[k] for k, _ in items[:items.index((kind, n))] if k in ("dots", "slab"))


POOL_ROWS = NFG * DOTS
ROWS_AT = [JUNK + GT * POOL_ROWS]
LOADS_AT = [[0] * SLOTS]
for _stage in range(GROUPS + 1):
    ROWS_AT.append(ROWS_AT[-1] + GT * per_tile(_stage))
for _stage in range(GROUPS):
    LOADS_AT.append([n + GT * len(range(slot, QUOTA[_stage], SLOTS))
                     for slot, n in enumerate(LOADS_AT[-1])])


def slots(stage):
    return SLOTS if stage < GROUPS else END_SLOTS


def slot_loads(stage, a, i):
    n = slots(stage)
    before = LOADS_AT[stage][i % n] if stage < GROUPS else 0
    return before + a * len(range(i % n, QUOTA[stage], n)) + i // n + 1


def dlrm_tower(nc, ids, tables, labels, ctx_t, w_score, b_rep, w5, b5, w6, b67_in, w7, w8, b8,
               v_i, v_j, top1, top1_ctx, bias1, top2, bias2, top3, ident_in, y_out):
    with ExitStack() as ctx:
        def sb(name, shape, dt=F32):
            return ctx.enter_context(nc.sbuf_tensor(name, shape, dt))

        def ps(name, shape):
            return ctx.enter_context(nc.psum_tensor(name, shape, F32))

        def sem(name):
            return ctx.enter_context(nc.semaphore(name))

        ident = sb("ident", [P, P])
        w5_sb = sb("w5_sb", [QC, QCN, EMB])
        w68 = sb("w68", [EC, ECN, EMB])
        w8_sb = sb("w8_sb", [EC, ECN, EMB])
        top1_sb = sb("top1_sb", [ZC, ZCN, TOP1])
        bias1_sb = sb("bias1_sb", [P, M1])
        top2_sb = sb("top2_sb", [P, M1, TOP2])
        bias2_sb = sb("bias2_sb", [P, M2])
        top3_sb = sb("top3_sb", [P, M2])
        pads = sb("pads", [P, FIELDS])
        g_all = sb("g_all", [P, CHUNKS])
        score_u = sb("score_u", [P, 2, EMB + 1])
        narrow = sb("narrow", [48, BATCH + TOP1])
        b5_sb = narrow[0:1, 0:EMB]
        bias8 = narrow[0:1, EMB:2 * EMB]
        b8_sb = narrow[0:1, 2 * EMB:3 * EMB]
        y_sb = narrow[0:1, BATCH:BATCH + GB]
        ones = narrow[0:1, BATCH + GB:BATCH + GB + P]
        ctx_sb = narrow[32:32 + CTX, 0:BATCH]
        top1c_sb = narrow[32:32 + CTX, BATCH:BATCH + TOP1]
        ids_sb = sb("ids_sb", [P, FIELDS], I32)
        x = sb("x", [P, FIELDS, EMB])
        absum = sb("absum", [P, FIELDS])
        columns = sb("columns", [P, 6, 2])
        top, ntop, exsum, rsum, tick = (columns[:, i, :] for i in range(5))
        abs_junk = sb("abs_junk", [P, 2, EMB], mybir.dt.bfloat16)
        score = sb("score", [P, 2, FIELDS])
        empty = sb("empty", [P, FIELDS], I32)
        ex = sb("ex", [P, 2, FIELDS])
        qa = sb("qa", [P, 2, 2, EMB])
        q = sb("q", [P, GT, 2 * EMB])
        hh = sb("hh", [P, GT, 2 * EMB])
        fine = sb("fine", [P, 3, FINE, GB])
        dup = sb("dup", [P, 2, GT, P])
        picked = sb("picked", [P, RING, GT, P])
        prod = sb("prod", [P, RING, FINE, GB])
        w7_sb = sb("w7_sb", [P, RING, FINE * EMB])
        ht = sb("ht", [EC, GT, ECN * P])
        out8 = sb("out8", [P, 3, GT, EMB])
        spare = fine[:, 2].rearrange("p m b -> p (m b)")
        diag = fine[:, 0].rearrange("p m b -> p (m b)")[:, 0:DIAGS * P].rearrange(
            "p (d b) -> p d b", d=DIAGS)
        qflat = q[:].rearrange("p t n -> p (t n)")
        qt = spare[0:QC, :].rearrange("p (t n) -> p t n", t=GT)
        f7s = qflat[:, 0:GT * EMB].rearrange("p (t e) -> p t e", t=GT)
        f7t = spare[0:EC, 0:GT * ECN * P].rearrange("p (t n) -> p t n", t=GT)
        zt = qflat[0:ZC, 0:ZCN * GB].rearrange("p (c b) -> p c b", c=ZCN)
        h1t = spare[:, 0:M1 * GB].rearrange("p (c b) -> p c b", c=M1)
        h2t = qflat[:, 0:M2 * GB].rearrange("p (c b) -> p c b", c=M2)
        lab = sb("lab", [P, SLOTS, SLAB, EMB])
        start = lab[:].rearrange("p s k e -> p (s k e)")
        at = [0]

        def early(rows, *dims):
            n = int(np.prod(dims))
            view = start[0:rows, at[0]:at[0] + n]
            at[0] += n
            return view.rearrange("p (a b) -> p a b", a=dims[0]) if len(dims) == 2 else view

        score_w = early(HIDDEN, 2, EMB + 1)
        score_v = early(HIDDEN, 2, P)
        w6t = early(EC, ECN, EMB)
        w8a = early(EC, ECN, EMB)
        b67 = early(EC, 2 * ECN)
        junk = sb("junk", [P, JUNK, EMB])
        z = sb("z", [P, 3, GT, LABELS])

        acc = [ps(f"acc{i}", [P, GT, 512]) for i in range(2)]
        coarse = ps("coarse", [P, RING, 512])
        misc = ps("misc", [P, 512])

        score_consts = sem("score_consts")
        consts = sem("consts")
        filled = sem("filled")
        g_ready = sem("g_ready")
        ids_loaded = sem("ids_loaded")
        gathered = [sem(f"gathered{j}") for j in range(NFG)]
        abs_done = sem("abs_done")
        pool_ticks = sem("pool_ticks")
        rows_done = sem("rows_done")
        exp1_done = sem("exp1_done")
        chain = sem("chain")
        ntop_ready = sem("ntop_ready")
        exp2_done = sem("exp2_done")
        wsum_done = sem("wsum_done")
        diag_ready = sem("diag_ready")
        diag_used = sem("diag_used")
        halves_added = sem("halves_added")
        q_ready = sem("q_ready")
        hh_ready = sem("hh_ready")
        cross_ready = sem("cross_ready")
        w7_loaded = [sem(f"w7_loaded{i}") for i in range(RING)]
        picked_ready = sem("picked_ready")
        coarse_ready = sem("coarse_ready")
        fine_ready = sem("fine_ready")
        chunk_ready = sem("chunk_ready")
        unit_used = sem("unit_used")
        pe_step = sem("pe_step")
        act_step = sem("act_step")
        out8_ready = sem("out8_ready")
        lab_loaded = [sem(f"lab_loaded{i}") for i in range(SLOTS)]
        end_loaded = [sem(f"end_loaded{i}") for i in range(END_SLOTS)]
        y_ready = sem("y_ready")
        y_stored = sem("y_stored")

        v_rows = prod[:].rearrange("p r m b -> p (r m b)")[:, 0:2 * CHUNKS * RANK].rearrange(
            "p (two n) -> p two n", two=2)
        label_rows = labels.rearrange("(t p) k e -> t p (k e)", p=P)
        id_rows = ids.rearrange("(t p) n -> t p n", p=P)

        DUP_ROWS = [P, P, P, 3 * THIRD]

        def slab_place(stage, i):
            if stage < GROUPS:
                return lab[:, i % SLOTS, :, :], lab_loaded[i % SLOTS]
            slot = i % END_SLOTS
            return x[:, slot * SLAB:(slot + 1) * SLAB, :], end_loaded[slot]

        def place_of(g, phase):
            return 2 if phase == 2 else (g + (0, 1, 0, 0)[phase]) % 2

        def slot_of(g, u):
            return (g * UNITS + u) % RING

        block = ctx.enter_context(nc.Block())

        @block.sync
        def _(sp):
            sp.dma_start(score_w, w_score).then_inc(score_consts, 16)
            sp.dma_start(score_v, b_rep).then_inc(score_consts, 16)
            sp.dma_start(v_rows[:, 0, :], v_i).then_inc(consts, 16)
            sp.dma_start(v_rows[:, 1, :], v_j).then_inc(consts, 16)
            for dst, src in ((ident[:], ident_in), (w5_sb[:], w5), (b5_sb, b5), (w6t, w6), (b67, b67_in),
                             (w8a, w8[:, 0:ECN, :]), (w8_sb[:], w8[:, ECN:2 * ECN, :]), (b8_sb, b8),
                             (top1_sb[:], top1), (top1c_sb, top1_ctx), (bias1_sb[:], bias1),
                             (top2_sb[:], top2), (bias2_sb[:], bias2), (top3_sb[:], top3),
                             (ctx_sb, ctx_t)):
                sp.dma_start(dst, src).then_inc(consts, 16)

            def load_w7(unit, u, slot):
                if not (isinstance(unit, int) and unit < RING):
                    sp.wait_ge(unit_used, CREDIT + unit - RING + 1)
                sp.dma_start(w7_sb[:, slot, :], w7[u]).then_inc(w7_loaded[slot], 16)

            def load_slab(stage, a, i):
                before = ROWS_AT[stage] + a * per_tile(stage)
                n = slots(stage)
                if i >= n:
                    used = before + rows_before(stage, "slab", i - n) + SLAB
                else:
                    used = before - (n - 1 - i) * SLAB
                    if stage == GROUPS:
                        used = pick(a, ROWS_AT[GROUPS - 1],
                                    ROWS_AT[GROUPS] + per_tile(GROUPS) - (n - 1 - i) * SLAB)
                sp.wait_ge(rows_done, used)
                group, s = LABEL_PLAN[stage][i]
                place, loaded = slab_place(stage, i)
                sp.dma_start(place.rearrange("p k e -> p (k e)"),
                             label_rows[group * GT + a, :, s * SLAB * EMB:(s + 1) * SLAB * EMB]
                             ).then_inc(loaded, 16)

            for u in range(RING):
                load_w7(u, u, u)
            with sp.Fori(1, UNITS // RING) as n:
                for i in range(RING):
                    load_w7(n * RING + i, n * RING + i, i)
            for u in range(UNITS - UNITS % RING, UNITS):
                load_w7(u, u, u % RING)
            for g in range(1, GROUPS):
                for u in range(UNITS):
                    load_w7(g * UNITS + u, u, slot_of(g, u))
                    a, step = divmod(u, TU)
                    for kind, i in PLANS[g][step] if a < GT else ():
                        if kind == "slab":
                            load_slab(g, a, i)
            with sp.Fori(0, GT) as a:
                for i in range(QUOTA[GROUPS]):
                    load_slab(GROUPS, a, i)

        @block.gpsimd
        def _(pool):
            def carry(tile_ticks, i):
                pool.wait_ge(pool_ticks, tile_ticks + i + 1)
                pool.tensor_tensor(tick[:, 1:2], tick[:, 0:1], tick[:, 0:1],
                                   ALU.add).then_inc(pool_ticks, 1)

            def tile(t, first=False, second=False):
                pool.dma_start(ids_sb[:], id_rows[t]).then_inc(ids_loaded, 16)
                pool.wait_ge(ids_loaded, 16 * (t + 1))
                if not first and not second:
                    pool.wait_ge(diag_used, GT * FIELDS)
                carry(0 if first else t * (NFG + 1) - NFG, 0)
                for n in range(FIELDS):
                    j = n // FG
                    if n % FG == 0 and not first:
                        pool.wait_ge(wsum_done, WSUMS * t - 2 * FIELDS + 2 * FG * (j + 1))
                        if second:
                            pool.wait_ge(diag_used, FG * (j + 1))
                        carry(t * (NFG + 1) - NFG, j + 1)
                    pool.indirect_dma_start(
                        out=x[:, n, :], out_offset=None, in_=tables[n],
                        in_offset=bass.IndirectOffsetOnAxis(ap=ids_sb[:, n:n + 1], axis=0)
                    ).then_inc(gathered[j], 16)
                for j in range(NFG):
                    pool.wait_ge(gathered[j], 16 * FG * (t + 1))

            pool.memset(tick, 0.0).then_inc(pool_ticks, 1)
            tile(0, first=True)
            tile(1, second=True)
            with pool.Fori(2, TILES) as t:
                tile(t)

        @block.vector
        def _(dve):
            dve.memset(ones, 1.0).then_inc(filled, 1)
            dve.memset(pads[:], PAD).then_inc(filled, 1)
            for r in range(JUNK):
                dve.memset(junk[:, r, :], 0.0).then_inc(rows_done, 1)
            dve.wait_ge(consts, 16 * CONSTS)
            dve.tensor_tensor(v_rows[:, 0, :], v_rows[:, 0, :], v_rows[:, 1, :],
                              ALU.mult).then_inc(g_ready, 1)
            dve.wait_ge(g_ready, 1)
            dve.tensor_reduce(g_all[:], v_rows[:, 0, :].rearrange("p (n r) -> p n r", r=RANK),
                              AX_X, ALU.add).then_inc(g_ready, 1)
            dve.wait_ge(g_ready, 2)
            dve.wait_ge(filled, 2)
            dve.wait_ge(act_step, 1)

            def row(count, i, in0, in1, out):
                dve.wait_ge(rows_done, count - JUNK + 1)
                dve.scalar_tensor_tensor(junk[:, i % JUNK, :], in0, 1.0, in1, ALU.mult, ALU.mult,
                                         accum_out=out).then_inc(rows_done, 1)

            def dots(t, count, half):
                if half % 2 == 0:
                    dve.wait_ge(gathered[half // 2], 16 * FG * (t + 1))
                for i in range(HALF):
                    n, head = (half * HALF + i) // 2, i % 2
                    row(count + i, half * HALF + i, x[:, n, :], score_u[:, head, 0:EMB],
                        score[:, head, n:n + 1])

            def then(t, k):
                dve.wait_ge(chain, t * CHAIN + k)

            def mask(t):
                dve.wait_ge(abs_done, FIELDS * (t + 1))
                dve.tensor_scalar(empty[:], absum[:], 0.0, None, ALU.is_equal).then_inc(chain, 1)
                dve.wait_ge(exp1_done, 2 * (t + 1))
                then(t, 1)
                dve.memset(rsum, 0.0).then_inc(chain, 1)
                for head in range(2):
                    dve.copy_predicated(score[:, head, :], empty[:], pads[:]).then_inc(chain, 1)
                then(t, 4)
                dve.tensor_reduce(top, score[:], AX_X, ALU.max).then_inc(chain, 1)
                then(t, 5)
                dve.tensor_scalar(ntop, top, -1.0, None, ALU.mult).then_inc(ntop_ready, 1)

            def normalise(t):
                dve.wait_ge(exp2_done, 2 * (t + 1))
                dve.reciprocal(rsum, exsum).then_inc(chain, 1)
                then(t, 6)
                for head in range(2):
                    dve.tensor_scalar(ex[:, head, :], ex[:, head, :], rsum[:, head:head + 1], None,
                                      ALU.mult).then_inc(chain, 1)
                then(t, 8)

            def weigh(t, k, n, head, part, made, counts):
                if k < 4:
                    dve.tensor_scalar(part, x[:, n, :], ex[:, head, n:n + 1], None,
                                      ALU.mult).then_inc(wsum_done, counts)
                else:
                    dve.wait_ge(wsum_done, WSUMS * t + made)
                    dve.scalar_tensor_tensor(part, x[:, n, :], ex[:, head, n:n + 1], part,
                                             ALU.mult, ALU.add).then_inc(wsum_done, counts)

            def wsums(t, half):
                for k in range(half * HALF, (half + 1) * HALF):
                    n, head = k // 2, k % 2
                    weigh(t, k, n, head, qa[:, n % 2, head, :], k - 3, 1)

            def pooled(t, a):
                dve.wait_ge(wsum_done, WSUMS * (t + 1))
                dve.tensor_tensor(q[:, a, :].rearrange("p (h e) -> p h e", h=2), qa[:, 0], qa[:, 1],
                                  ALU.add).then_inc(q_ready, 1)
                dve.wait_ge(q_ready, t + 1)

            def wsums_even(t):
                for k in range(FIELDS):
                    n, head = k // 2 * 2, k % 2
                    weigh(t, k, n, head, qa[:, k // 2 % 2, head, :], 2 * (k - 3), 2)

            def pooled_with(t):
                dve.wait_ge(wsum_done, WSUMS * (t + 1))
                dve.tensor_tensor(qa[:, 0], qa[:, 0], qa[:, 1], ALU.add).then_inc(halves_added, 1)
                dve.wait_ge(halves_added, t + 1)
                dve.wait_ge(diag_used, FIELDS * (t + 1))
                dve.tensor_tensor(q[:, t, :].rearrange("p (h e) -> p h e", h=2),
                                  qa[:, 0], acc[1][:, :, 0:EMB], ALU.add).then_inc(q_ready, 1)
                dve.wait_ge(q_ready, t + 1)

            def make_cross(g, a, i):
                here, there = i, TU + i
                unit = g * UNITS + a * TU + i
                slot = pick(a, slot_of(g, here), slot_of(g, there))
                phases = [phase_of(here), phase_of(min(there, UNITS - 1))]
                if here in PHASE_AT or there in PHASE_AT:
                    dve.wait_ge(fine_ready, FINE_COPIES * (4 * g + 1 + pick(a, *phases)))
                dve.wait_ge(coarse_ready, unit + 1)
                dve.wait_ge(unit_used, CREDIT + unit - RING + 1)
                window = coarse[:, bass.ds(slot, 1), 0:GB]
                window = bass.AP(tensor=window.tensor, offset=window.offset,
                                 ap=[list(window.ap[0]), [0, FINE], [1, GB]])
                fines = fine[:, bass.ds(pick(a, *(place_of(g, phase) for phase in phases)), 1), :, :]
                out = prod[:, bass.ds(slot, 1), :, :]
                dve.tensor_tensor(out.rearrange("p o m b -> p (o m) b"),
                                  fines.rearrange("p o m b -> p (o m) b"), window,
                                  ALU.mult).then_inc(cross_ready, 1)

            def slab(stage, a, i, count):
                group, s = LABEL_PLAN[stage][i]
                if i == 0 or LABEL_PLAN[stage][i - 1][0] != group:
                    dve.wait_ge(out8_ready, group + 1)
                place, loaded = slab_place(stage, i)
                dve.wait_ge(loaded, 16 * slot_loads(stage, a, i))
                for k in range(SLAB):
                    row(count + k, k, place[:, k, :], out8[:, group % 3, a, :],
                        z[:, group % 3, a, s * SLAB + k:s * SLAB + k + 1])

            def stage(g):
                make_cross(g, 0, 0)
                with dve.Fori(0, GT) as a:
                    before = ROWS_AT[g] + a * per_tile(g)
                    t = (g + 1) * GT + a
                    for step in range(TU):
                        make_cross(g, a, step + 1)
                        for kind, n in PLANS[g][step]:
                            if kind == "slab":
                                slab(g, a, n, before + rows_before(g, kind, n))
                            elif kind == "dots":
                                dots(t, before + rows_before(g, kind, n), n)
                            elif kind == "mask":
                                mask(t)
                            elif kind == "normalise":
                                normalise(t)
                            elif kind == "wsums":
                                wsums(t, n)
                            elif kind == "pooled":
                                pooled(t, a)

            with dve.Fori(0, GT) as a:
                for half in range(2 * NFG):
                    dots(a, JUNK + a * POOL_ROWS + half * HALF, half)
                mask(a)
                normalise(a)
                wsums_even(a)
                pooled_with(a)
            dve.engine_nop().then_inc(unit_used, CREDIT)
            for g in range(GROUPS):
                stage(g)
            with dve.Fori(0, GT) as a:
                for i in range(QUOTA[GROUPS]):
                    slab(GROUPS, a, i, ROWS_AT[GROUPS] + a * per_tile(GROUPS) +
                         rows_before(GROUPS, "slab", i))

        class Steps:

            def __init__(self):
                self.pe = self.act = self.fine = 0

        def bursts_of(stage):
            names = []
            if stage >= 1:
                names += [("f7", stage - 1), ("out8", stage - 1)]
            if stage < GROUPS:
                names += [("ht", stage)]
            if stage == GROUPS:
                groups = range(GROUPS - 3, GROUPS)
            else:
                groups = range(stage - 3, stage - 2) if stage >= 3 else ()
            for g in groups:
                names += [(n, (g, stage)) for n in ("zt", "h1", "h2", "y")]
            return names

        AHEAD = 3
        FIRST_BURST, BURST_STEP = 2, AHEAD + 1
        LAST = UNITS - 5
        POOLED_AT = LAST * FINE
        H_AT = POOLED_AT + 4
        FIRST_FINE_AT = [H_AT + 4 + 4 * n for n in range(FINE_COPIES)]
        COARSE_AT = FIRST_FINE_AT[-1] + 4
        PICKS_AT = [H_AT + 3, H_AT + 7, H_AT + 12]
        HEAD = 6
        FINE_AT = {PHASE_AT[1] - 6: 1, PHASE_AT[2] - 9: 2, PHASE_AT[2] - 6: 3}

        def plain(engine, run, g, u0, u1):
            whole = (u1 - u0) // RING
            if whole:
                with engine.Fori(0, whole) as n:
                    for i in range(RING):
                        run(u0 + n * RING + i, slot_of(g, u0 + i))
            for u in range(u0 + whole * RING, u1):
                run(u, slot_of(g, u))

        @block.tensor
        def _(pe):
            steps = Steps()

            def done(ins):
                ins.then_inc(pe_step, 1)
                steps.pe += 1

            def after_copies(n):
                steps.act += n
                pe.wait_ge(act_step, steps.act)

            def misc_free():
                pe.wait_ge(act_step, steps.act)
                if steps.fine:
                    pe.wait_ge(fine_ready, steps.fine)

            def turn_coarse(g, u, slot, rows=P):
                unit = g * UNITS + u
                pe.wait_ge(picked_ready, unit + 1)
                if not (isinstance(unit, int) and unit < RING):
                    pe.wait_ge(cross_ready, unit - RING + 1)
                for t in range(GT):
                    last = pe.transpose(coarse[0:rows, slot, t * P:(t + 1) * P],
                                        picked[:, slot, t, 0:rows], ident[:])
                last.then_inc(coarse_ready, 1)

            def turn_fine(phase, n):
                ms = range(2 * n, min(2 * n + 2, FINE))
                if phase >= 2:
                    steps.act += len(ms)
                misc_free()
                for m in ms:
                    for t in range(GT):
                        at = (m % 2 * GT + t) * P
                        if phase < 2:
                            start = (EMB, P)[phase] - m
                            last = pe.transpose(misc[:, at:at + P], hh[:, t, start:start + P],
                                                ident[:])
                        else:
                            rows = DUP_ROWS[phase]
                            last = pe.transpose(misc[0:rows, at:at + P], dup[:, m % 2, t, 0:rows],
                                                ident[:])
                done(last)
                steps.fine += 1

            def run_unit(g, u, slot, hooks={}, first=False, last_unit=False, rows=P, next_rows=P):
                unit = g * UNITS + u
                pe.wait_ge(w7_loaded[slot], w7_count(unit, slot))
                for m in range(FINE):
                    pe.wait_ge(chunk_ready, unit * FINE + m + 1)
                    for t in range(GT):
                        last = pe.matmul(acc[g % 2][:, t, 0:EMB], prod[0:rows, slot, m, t * P:(t + 1) * P],
                                         w7_sb[0:rows, slot, m * EMB:(m + 1) * EMB],
                                         start=first and m == 0, stop=last_unit and m == FINE - 1)
                    if m == FINE - 1:
                        last.then_inc(unit_used, 1)
                    if m == 0 and not (isinstance(u, int) and u + 2 >= UNITS):
                        turn_coarse(g, u + 2, (slot + 2) % RING, next_rows)
                    for hook in hooks.get(m, ()):
                        hook()

            def run(g, u0, u1, hooks={}):
                for u in range(u0, u1):
                    run_unit(g, u, slot_of(g, u), {m: hooks[u, m] for m in range(FINE) if (u, m) in hooks},
                             first=u == 0, last_unit=u == UNITS - 1, rows=PHASE_ROWS[phase_of(u)],
                             next_rows=PHASE_ROWS[phase_of(u + 2)])

            def w7_count(unit, slot):
                return 16 * ((unit - slot) // RING + 1)

            def pooled_turned(g):
                pe.wait_ge(q_ready, GT * (g + 1))
                misc_free()
                if g >= 2:
                    pe.wait_ge(out8_ready, g - 1)
                bank = acc[g % 2]
                for t in range(GT):
                    for c in range(QCN):
                        dst = bank[0:QC, t, c * P:(c + 1) * P] if c < 4 else misc[0:QC, t * P:(t + 1) * P]
                        last = pe.transpose(dst, q[:, t, c * QC:(c + 1) * QC], ident[:])
                done(last)

            def make_h(g):
                after_copies(2)
                for t in range(GT):
                    dst = acc[g % 2][:, t, 0:EMB]
                    for c in range(QCN):
                        pe.matmul(dst, qt[:, t, c * P:(c + 1) * P], w5_sb[:, c, :],
                                  start=c == 0, stop=False)
                    last = pe.matmul(dst, ones, b5_sb, start=False, stop=True)
                done(last)

            def f7_turned(g):
                after_copies(1)
                for t in range(GT):
                    for c in range(ECN):
                        last = pe.transpose(acc[g % 2][0:EC, t, c * P:(c + 1) * P],
                                            f7s[:, t, c * EC:(c + 1) * EC], ident[:])
                done(last)

            def make_out8(g):
                after_copies(1)
                for t in range(GT):
                    dst = acc[g % 2][:, t, 0:EMB]
                    for c in range(ECN):
                        pe.matmul(dst, ht[:, t, c * P:(c + 1) * P], w68[:, c, :],
                                  start=c == 0, stop=False)
                        pe.matmul(dst, f7t[:, t, c * P:(c + 1) * P], w8_sb[:, c, :],
                                  start=False, stop=False)
                    last = pe.matmul(dst, ones, bias8, start=False, stop=True)
                done(last)

            def h_turned(g):
                pe.wait_ge(hh_ready, 2 * (g + 1))
                if g:
                    pe.wait_ge(out8_ready, g)
                bank = acc[(g + 1) % 2]
                for t in range(GT):
                    for c in range(ECN):
                        last = pe.transpose(bank[0:EC, t, c * P:(c + 1) * P],
                                            hh[:, t, c * EC:(c + 1) * EC], ident[:])
                done(last)
                steps.act += 1

            def z_turned(at):
                g, stage = at
                last = max(i for i, slabs in enumerate(LABEL_PLAN) if g in (of for of, _ in slabs))
                pe.wait_ge(rows_done, ROWS_AT[last + 1])
                misc_free()
                for c in range(ZCN):
                    for t in range(GT):
                        last = pe.transpose(misc[0:ZC, (c * GT + t) * P:(c * GT + t + 1) * P],
                                            z[:, g % 3, t, c * ZC:(c + 1) * ZC], ident[:])
                done(last)

            def make_h1(at):
                g, stage = at
                """the first top layer over [z, context], turned"""
                after_copies(1)
                pe.wait_ge(out8_ready, stage)
                if g:
                    pe.wait_ge(y_ready, g)
                for m in range(M1):
                    dst = acc[(stage + 1) % 2][:, m // 2, m % 2 * GB:(m % 2 + 1) * GB]
                    for c in range(ZCN):
                        pe.matmul(dst, top1_sb[:, c, m * P:(m + 1) * P], zt[:, c, :],
                                  start=c == 0, stop=False)
                    last = pe.matmul(dst, top1c_sb[:, m * P:(m + 1) * P],
                                     ctx_sb[:, g * GB:(g + 1) * GB], start=False, stop=True)
                done(last)

            def make_h2(at):
                after_copies(M1)
                for m in range(M2):
                    for c in range(M1):
                        last = pe.matmul(misc[:, m * GB:(m + 1) * GB], top2_sb[:, c, m * P:(m + 1) * P],
                                         h1t[:, c, :], start=c == 0, stop=c == M1 - 1)
                done(last)

            def make_y(at):
                g, stage = at
                after_copies(M2)
                for c in range(M2):
                    last = pe.matmul(acc[(stage + 1) % 2][0:1, 0, 0:GB], top3_sb[:, c:c + 1], h2t[:, c, :],
                                     start=c == 0, stop=c == M2 - 1)
                done(last)

            BURSTS = {"f7": f7_turned, "out8": make_out8, "ht": h_turned,
                      "zt": z_turned, "h1": make_h1, "h2": make_h2, "y": make_y}

            pe.wait_ge(score_consts, 32)
            for head in range(2):
                last = pe.matmul(acc[1][:, head, 0:EMB + 1], score_v[:, head, :], score_w[:, head, :],
                                 start=True, stop=True)
            done(last)
            steps.act += 1
            pe.wait_ge(consts, 16 * CONSTS)
            pe.wait_ge(filled, 2)
            for m in range(ECN):
                for c in range(ECN):
                    last = pe.matmul(coarse[0:EC, m, 0:EMB], w6t[:, c, m * EC:(m + 1) * EC], w8a[:, c, :],
                                     start=c == 0, stop=c == ECN - 1)
            for c in range(ECN):
                pe.matmul(misc[0:1, 0:EMB], b67[:, c:c + 1], w8a[:, c, :], start=c == 0, stop=False)
                pe.matmul(misc[0:1, 0:EMB], b67[:, ECN + c:ECN + c + 1], w8_sb[:, c, :],
                          start=False, stop=False)
            done(pe.matmul(misc[0:1, 0:EMB], ones[:, 0:1], b8_sb, start=False, stop=True))
            steps.act += ECN + 1
            with pe.Fori(0, GT) as t:
                for k in range(FIELDS):
                    n, head = k // 2 * 2 + 1, k % 2
                    pe.wait_ge(diag_ready, FIELDS * t + k + 1)
                    pe.matmul(acc[1][:, head, 0:EMB], diag[:, k % DIAGS, :], x[:, n, :],
                              start=k < 2, stop=k >= FIELDS - 2).then_inc(diag_used, 1)
            pooled_turned(0)
            make_h(0)

            def turn_first(g):
                pe.wait_ge(hh_ready, 2 * (g + 1))
                for n in range(FINE_COPIES):
                    turn_fine(0, n)
                first_coarse(g)

            def first_coarse(g):
                for u in range(2):
                    turn_coarse(g, u, slot_of(g, u))

            turn_first(0)
            for g in range(GROUPS):
                hooks = {}
                for i, (name, of) in enumerate(bursts_of(g)):
                    hooks[divmod(FIRST_BURST + BURST_STEP * i, FINE)] = [
                        lambda name=name, of=of: BURSTS[name](of)]
                for at, phase in FINE_AT.items():
                    for n in range(FINE_COPIES):
                        hooks[at + n, 2] = [lambda phase=phase, n=n: turn_fine(phase, n)]
                if g + 1 < GROUPS:
                    hooks[divmod(POOLED_AT, FINE)] = [lambda: pooled_turned(g + 1)]
                    hooks[divmod(H_AT, FINE)] = [lambda: make_h(g + 1)]
                    for n in range(FINE_COPIES):
                        hooks[divmod(FIRST_FINE_AT[n], FINE)] = [lambda n=n: (
                            n == 0 and pe.wait_ge(hh_ready, 2 * (g + 2)), turn_fine(0, n))]
                    hooks[divmod(COARSE_AT, FINE)] = [lambda: first_coarse(g + 1)]
                one = lambda u, slot: run_unit(g, u, slot)
                run(g, 0, HEAD, hooks)
                plain(pe, one, g, HEAD, PHASE_AT[1] - 6)
                run(g, PHASE_AT[1] - 6, PHASE_AT[1] - 3, hooks)
                plain(pe, one, g, PHASE_AT[1] - 3, PHASE_AT[2] - 9)
                run(g, PHASE_AT[2] - 9, PHASE_AT[3], hooks)
                plain(pe, lambda u, slot: run_unit(g, u, slot, rows=PHASE_ROWS[3],
                                                   next_rows=PHASE_ROWS[3]), g, PHASE_AT[3], LAST)
                run(g, LAST, UNITS, hooks)
            for name, of in bursts_of(GROUPS):
                BURSTS[name](of)

        @block.scalar
        def _(act):
            steps = Steps()

            def copies(*made, wait=True):
                if wait:
                    steps.pe += 1
                    act.wait_ge(pe_step, steps.pe)
                for out, in_, func, kw in made:
                    act.activation(out, in_, func, **kw).then_inc(act_step, 1)
                    steps.act += 1

            def run_unit(g, u, slot, hooks={}):
                unit = g * UNITS + u
                act.wait_ge(cross_ready, unit + 1)
                if not (isinstance(u, int) and u + RING >= UNITS):
                    pick_window(g, u + RING, phase_now[0], slot)
                for m in range(FINE):
                    act.activation(prod[:, slot, m, :], prod[:, slot, m, :], ACT.Copy,
                                   scale=g_all[:, bass.ds(u * FINE + m, 1)]).then_inc(chunk_ready, 1)
                    for hook in hooks.get(m, ()):
                        hook()

            phase_now = [0]

            def pick_window(g, u, phase, slot):
                if not (isinstance(g, int) and isinstance(u, int) and g * UNITS + u < RING):
                    act.wait_ge(coarse_ready, g * UNITS + u - RING + 1)
                k = u - PHASE_AT[phase]
                if phase < 2:
                    cols = hh[:, :, bass.ds(P * phase + FINE * k + 1, P)]
                    out = picked[:, slot, :, :]
                else:
                    start, windows, width = ((2 * P + THIRD, COARSE, LEFT), (2 * P, 3, THIRD))[phase - 2]
                    cols = hh[:, :, bass.ds(start + windows * FINE * k + 1, width)]
                    cols = bass.AP(tensor=cols.tensor, offset=cols.offset,
                                   ap=[list(cols.ap[0]), list(cols.ap[1]), [FINE, windows], [1, width]])
                    out = picked[:, slot, :, 0:windows * width].rearrange(
                        "p t (k n) -> p t k n", k=windows)
                act.activation(out, cols, ACT.Copy).then_inc(picked_ready, 1)

            def run(g, u0, u1, hooks={}):
                for u in range(u0, u1):
                    phase_now[0] = phase_of(min(u + RING, UNITS - 1))
                    run_unit(g, u, slot_of(g, u), {m: hooks[u, m] for m in range(FINE) if (u, m) in hooks})

            def sum_abs(t, j):
                act.wait_ge(gathered[j], 16 * FG * (t + 1))
                for n in range(j * FG, (j + 1) * FG):
                    if FIELDS * t + n >= 2:
                        act.wait_ge(abs_done, FIELDS * t + n - 1)
                    act.activation(abs_junk[:, n % 2, :], x[:, n, :], ACT.Abs,
                                   accum_out=absum[:, n:n + 1]).then_inc(abs_done, 1)

            def abs_hooks(g, a, j):
                t = (g + 1) * GT + a
                rows = ROWS_AT[g] + a * per_tile(g) + j * rows_before(g, "dots", 2)

                def one(n):
                    if n == 0:
                        act.wait_ge(rows_done, rows + 1)
                    act.wait_ge(abs_done, FIELDS * t + j * FG + n - 1)
                    at = bass.ds(j * FG + n, 1)
                    act.activation(abs_junk[:, n % 2, :], x[:, at, :].rearrange("p o e -> p (o e)"),
                                   ACT.Abs, accum_out=absum[:, at]).then_inc(abs_done, 1)
                return {divmod(3 * FINE - FG + n, FINE): lambda n=n: one(n) for n in range(FG)}

            def abs_loop(g, a, j0):
                with act.Fori(j0, NFG) as j:
                    hooks = abs_hooks(g, a, j)
                    for i in range(3):
                        run_unit(g, a * TU + 3 * j + i, slot_of(g, a * TU + i),
                                 {m: [hooks[i, m]] for m in range(FINE) if (i, m) in hooks})

            def exp_scores(t, rows):
                act.wait_ge(rows_done, rows)
                for head in range(2):
                    act.activation(score[:, head, :], score[:, head, :], ACT.Exp,
                                   bias=score_u[:, head, EMB:EMB + 1]).then_inc(exp1_done, 1)

            def exp_softmax(t):
                act.wait_ge(ntop_ready, t + 1)
                for head in range(2):
                    act.activation(ex[:, head, :], score[:, head, :], ACT.Exp,
                                   bias=ntop[:, head:head + 1],
                                   accum_out=exsum[:, head:head + 1]).then_inc(exp2_done, 1)

            def make_diags(t):
                act.wait_ge(chain, CHAIN * (t + 1))
                if t:
                    act.wait_ge(q_ready, t)
                for k in range(FIELDS):
                    n, head = k // 2 * 2 + 1, k % 2
                    count = FIELDS * t + k
                    if count >= DIAGS:
                        act.wait_ge(diag_used, count - DIAGS + 1)
                    act.activation(diag[:, k % DIAGS, :], ident[:], ACT.Copy,
                                   scale=ex[:, head, n:n + 1]).then_inc(diag_ready, 1)

            def after_pooled_turned(g):
                bank = acc[g % 2]
                copies((qt[:, :, 0:4 * P], bank[0:QC, :, 0:4 * P], ACT.Copy, {}),
                       (qt[:, :, 4 * P:5 * P], misc[0:QC, 0:GT * P].rearrange("p (t b) -> p t b", t=GT),
                        ACT.Copy, {}))

            def after_h(g):
                steps.pe += 1
                act.wait_ge(pe_step, steps.pe)
                if g:
                    act.wait_ge(picked_ready, g * UNITS)
                for half in range(2):
                    act.activation(hh[:, :, half * EMB:(half + 1) * EMB], acc[g % 2][:, :, 0:EMB],
                                   ACT.Copy).then_inc(hh_ready, 1)
                act.wait_ge(hh_ready, 2 * (g + 1))

            def before_f7_turned(g):
                act.wait_ge(unit_used, CREDIT + (g + 1) * UNITS)
                copies((f7s, acc[g % 2][:, :, 0:EMB], ACT.Copy, {}), wait=False)

            def after_f7_turned(g):
                copies((f7t, acc[g % 2][0:EC, :, 0:ECN * P], ACT.Copy, {}))

            def after_out8(g):
                if g >= 3:
                    act.wait_ge(rows_done, ROWS_AT[g])
                steps.pe += 1
                act.wait_ge(pe_step, steps.pe)
                act.activation(out8[:, g % 3], acc[g % 2][:, :, 0:EMB], ACT.Copy).then_inc(out8_ready, 1)

            def after_h_turned(g):
                copies((ht[:], acc[(g + 1) % 2][0:EC, :, 0:ECN * P], ACT.Copy, {}))

            def after_z_turned(at):
                copies((zt, misc[0:ZC, :].rearrange("p (c b) -> p c b", c=ZCN), ACT.Copy, {}))

            def after_h1(at):
                g, stage = at
                copies(*((h1t[:, m, :], acc[(stage + 1) % 2][:, m // 2, m % 2 * GB:(m % 2 + 1) * GB],
                          ACT.Relu, dict(bias=bias1_sb[:, m:m + 1])) for m in range(M1)))

            def after_h2(at):
                copies(*((h2t[:, m, :], misc[:, m * GB:(m + 1) * GB], ACT.Relu,
                          dict(bias=bias2_sb[:, m:m + 1])) for m in range(M2)))

            def after_y(at):
                g, stage = at
                steps.pe += 1
                act.wait_ge(pe_step, steps.pe)
                if g:
                    act.wait_ge(y_stored, 16 * g)
                act.activation(y_sb, acc[(stage + 1) % 2][0:1, 0, 0:GB], ACT.Copy).then_inc(y_ready, 1)
                act.wait_ge(y_ready, g + 1)
                act.dma_start(y_out[g * GB:(g + 1) * GB, :].rearrange("b o -> o b"),
                              y_sb).then_inc(y_stored, 16)

            AFTER = {"f7": after_f7_turned, "out8": after_out8, "ht": after_h_turned,
                     "zt": after_z_turned, "h1": after_h1, "h2": after_h2, "y": after_y}

            steps.pe += 1
            act.wait_ge(pe_step, steps.pe)
            act.activation(score_u[:], acc[1][:, :, 0:EMB + 1], ACT.Copy).then_inc(act_step, 1)
            steps.act += 1
            act.wait_ge(consts, 16 * CONSTS)
            copies(*((w68[:, m, :], coarse[0:EC, m, 0:EMB], ACT.Copy, {}) for m in range(ECN)),
                   (bias8, misc[0:1, 0:EMB], ACT.Copy, {}))
            for t in range(GT):
                for j in range(NFG):
                    sum_abs(t, j)
                exp_scores(t, JUNK + (t + 1) * POOL_ROWS)
                exp_softmax(t)
                make_diags(t)
            def copy_fine(g, phase, n):
                steps.pe += 1
                act.wait_ge(pe_step, steps.pe)
                ms = range(2 * n, min(2 * n + 2, FINE))
                rows = DUP_ROWS[phase]
                act.activation(fine[0:rows, place_of(g, phase), ms[0]:ms[-1] + 1, :],
                               misc[0:rows, 0:len(ms) * GB].rearrange("p (m b) -> p m b", b=GB),
                               ACT.Copy).then_inc(fine_ready, 1)

            def repeat_fine(phase, n):
                start, width = ((2 * P + THIRD, LEFT), (2 * P, THIRD))[phase - 2]
                times = DUP_ROWS[phase] // width
                for m in range(2 * n, min(2 * n + 2, FINE)):
                    cols = hh[:, :, bass.ds(start - m, width)]
                    cols = bass.AP(tensor=cols.tensor, offset=cols.offset,
                                   ap=[list(cols.ap[0]), list(cols.ap[1]), [0, times], [1, width]])
                    act.activation(dup[:, m % 2, :, 0:times * width].rearrange(
                        "p t (k n) -> p t k n", k=times), cols, ACT.Copy).then_inc(act_step, 1)

            after_pooled_turned(0)
            after_h(0)
            for u in range(RING):
                pick_window(0, u, 0, slot_of(0, u))
            for n in range(FINE_COPIES):
                copy_fine(0, 0, n)
            act.wait_ge(g_ready, 2)
            for g in range(GROUPS):
                more = g + 1 < GROUPS
                hooks = {}
                for i, (name, of) in enumerate(bursts_of(g)):
                    hooks[divmod(FIRST_BURST + BURST_STEP * i + AHEAD, FINE)] = [
                        lambda name=name, of=of: AFTER[name](of)]
                for at, phase in FINE_AT.items():
                    for n in range(FINE_COPIES):
                        hooks[at + n, 4] = [lambda phase=phase, n=n: copy_fine(g, phase, n)]
                        if phase >= 2:
                            hooks[at + n, 0] = [lambda phase=phase, n=n: repeat_fine(phase, n)]
                if g:
                    hooks[0, FIRST_BURST - 1] = [lambda: before_f7_turned(g - 1)]
                if more:
                    for j in range(HEAD // 3):
                        for (i, m), hook in abs_hooks(g, 0, j).items():
                            hooks.setdefault((3 * j + i, m), []).append(hook)
                    for a in range(GT):
                        rows = ROWS_AT[g] + a * per_tile(g) + \
                            rows_before(g, "dots", 2 * NFG - 1) + HALF
                        t = (g + 1) * GT + a
                        hooks[a * TU + 3 * NFG, 1] = [lambda t=t, rows=rows: exp_scores(t, rows)]
                        hooks[a * TU + 3 * NFG + 1, 1] = [lambda t=t: exp_softmax(t)]
                    hooks[divmod(POOLED_AT + AHEAD, FINE)] = [lambda: after_pooled_turned(g + 1)]
                    hooks[divmod(H_AT + 2, FINE)] = [lambda: after_h(g + 1)]
                    for u in range(RING):
                        hooks.setdefault(divmod(PICKS_AT[u], FINE), []).append(
                            lambda u=u: pick_window(g + 1, u, 0, slot_of(g + 1, u)))
                    for n in range(FINE_COPIES):
                        hooks.setdefault(divmod(FIRST_FINE_AT[n] + 2, FINE), []).append(
                            lambda n=n: copy_fine(g + 1, 0, n))
                run(g, 0, HEAD, hooks)
                one = lambda u, slot: run_unit(g, u, slot)
                if more:
                    abs_loop(g, 0, HEAD // 3)
                    run(g, 3 * NFG, 3 * NFG + 2, hooks)
                    plain(act, one, g, 3 * NFG + 2, PHASE_AT[1] - 6)
                    run(g, PHASE_AT[1] - 6, PHASE_AT[1] - 3, hooks)
                    phase_now[0] = 1
                    plain(act, one, g, PHASE_AT[1] - 3, TU)
                    abs_loop(g, 1, 0)
                    run(g, TU + 3 * NFG, PHASE_AT[3] - 3, hooks)
                else:
                    plain(act, one, g, HEAD, PHASE_AT[1] - 6)
                    run(g, PHASE_AT[1] - 6, PHASE_AT[1] - 3, hooks)
                    phase_now[0] = 1
                    plain(act, one, g, PHASE_AT[1] - 3, PHASE_AT[2] - 9)
                    run(g, PHASE_AT[2] - 9, PHASE_AT[3] - 3, hooks)
                phase_now[0] = 3
                plain(act, one, g, PHASE_AT[3] - 3, LAST)
                run(g, LAST, UNITS, hooks)
            before_f7_turned(GROUPS - 1)
            for name, of in bursts_of(GROUPS):
                AFTER[name](of)
            act.wait_ge(y_stored, 16 * GROUPS)


def pair_order():
    u, m, p = np.meshgrid(np.arange(UNITS), np.arange(FINE), np.arange(P), indexing="ij")
    phase = np.searchsorted(PHASE_AT, u, side="right") - 1
    k = np.choose(phase, [u, u - PHASE_AT[1], p // LEFT, 3 * (u - PHASE_AT[3]) + p // THIRD])
    d = FINE * k + m + 1
    i = (np.choose(phase, [p, P + p, 2 * P + THIRD + p % LEFT, 2 * P + p % THIRD]) - m) % EMB
    j = (i + d) % EMB
    lo, hi = np.minimum(i, j), np.maximum(i, j)
    once = (p < np.choose(phase, PHASE_ROWS)) & ~((d == DISTANCES) & (i >= DISTANCES))
    return lo, hi, once


_OUT = ((BATCH, 1), "float32")


def kernel(**inputs):
    import concourse.bacc as _bacc
    from concourse.bass_utils import run_bass_kernel_spmd as _run

    a = {k: np.asarray(v) for k, v in inputs.items()}
    lo, hi, once = pair_order()
    row_of = lo * EMB - lo * (lo + 1) // 2 - lo - 1 + hi
    w7 = np.zeros((UNITS, FINE, P, EMB), np.float32)
    w7[once] = a["L0_rec_w7"][row_of[once]]
    w7 = w7.transpose(0, 2, 1, 3)

    def pair_rows(idx):
        out = np.zeros((UNITS, FINE, P, RANK), np.float32)
        out[once] = a["L0_rec_v"][idx[once]]
        return out.transpose(2, 0, 1, 3).reshape(P, -1)

    def split(w, rows):
        return w.reshape(-1, rows, w.shape[-1]).transpose(1, 0, 2)

    def columns(b, rows):
        return b.reshape(-1, rows).T

    w_score = np.stack([np.concatenate([a["L0_rec_w1"], a["L0_rec_b1"][None]]).T,
                        np.concatenate([a["L0_rec_w3"], a["L0_rec_b3"][None]]).T], 1)
    v_score = np.stack([np.repeat(a["L0_rec_w2"], P, 1), np.repeat(a["L0_rec_w4"], P, 1)], 1)
    arrays = {
        "ids": a["ids"], **{f"tbl_{n}": a[f"tbl_{n}"] for n in range(FIELDS)},
        "labels": a["r_label_embedding"], "ctx_t": a["dense_ctx"].T,
        "w_score": w_score, "v_score": v_score,
        "w5": split(a["L0_rec_w5"], QC), "b5": a["L0_rec_b5"][None],
        "w6t": split(a["L0_rec_w6"].T, EC),
        "b67": np.concatenate([columns(a["L0_rec_b6"], EC), columns(a["L0_rec_b7"], EC)], 1),
        "w7": w7.reshape(UNITS, P, -1),
        "w8": split(a["L0_rec_w8"], EC), "b8": a["L0_rec_b8"][None],
        "v_i": pair_rows(lo), "v_j": pair_rows(hi),
        "top1": split(a["W_top1"][:LABELS], ZC), "top1_ctx": a["W_top1"][LABELS:],
        "bias1": columns(a["b_top1"], P), "top2": split(a["W_top2"], P),
        "bias2": columns(a["b_top2"], P), "top3": columns(a["W_top3"], P),
        "ident": np.eye(P, dtype=np.float32),
    }
    nc = _bacc.Bacc("TRN2", target_bir_lowering=False, num_devices=1)
    sent, aps = {}, {}
    for name, array in arrays.items():
        array = np.ascontiguousarray(array)
        sent[f"in_{name}"] = array
        aps[name] = nc.dram_tensor(f"in_{name}", array.shape, mybir.dt.from_np(array.dtype),
                                   kind="ExternalInput").ap()
    shape, dtype = _OUT
    y = nc.dram_tensor("out_y", shape, mybir.dt.from_np(np.dtype(dtype)), kind="ExternalOutput").ap()
    g = aps
    dlrm_tower(nc, g["ids"], [g[f"tbl_{n}"] for n in range(FIELDS)], g["labels"], g["ctx_t"],
               g["w_score"], g["v_score"], g["w5"], g["b5"], g["w6t"], g["b67"], g["w7"],
               g["w8"], g["b8"], g["v_i"], g["v_j"], g["top1"], g["top1_ctx"], g["bias1"],
               g["top2"], g["bias2"], g["top3"], g["ident"], y)
    return _run(nc, [sent], core_ids=[0]).results[0]["out_y"]
```
